# Optimizing a Trainium2 kernel written in Bass

```python
import numpy as np
import jax
import jax.numpy as jnp

def _softmax(x, axis=-1):
    return jax.nn.softmax(x, axis=axis)

def _gelu(x):
    return jax.nn.gelu(x, approximate=True)

def _silu(x):
    return jax.nn.silu(x)

def _sigmoid(x):
    return jax.nn.sigmoid(x)

def _layernorm(x, axis=-1, eps=1e-05):
    m = jnp.mean(x, axis=axis, keepdims=True)
    v = jnp.var(x, axis=axis, keepdims=True)
    return (x - m) / jnp.sqrt(v + eps)

def _scatter_add(tgt, idx, src, axis=0):
    return tgt.at[idx].add(src)

def _segment_sum(src, seg, n):
    return jax.ops.segment_sum(src, seg, n)
kernel_name = 'mk_dlrm_tower_d1_rec_r8_0cafbf'

def setup_inputs(seed: int=0):
    np.random.seed(seed)
    _w = jnp.asarray

    def _rec_inputs():
        import jax
        import jax.numpy as jnp
        _tk = jax.random.key(seed)
        dense_ctx = jax.random.normal(jax.random.fold_in(_tk, 190), (1024, 16), jnp.float32)
        ids = jnp.stack([jax.random.randint(jax.random.fold_in(_tk, 200 + f), (1024,), 0, v, jnp.int32) for f, v in enumerate([1000, 1250, 1000, 1250, 12500, 1250, 1250, 12500, 1250, 125000, 125000, 125000, 1000, 125000, 1000, 1250, 1000, 1250, 1250, 125000, 1000, 125000, 1250, 1000, 125000, 1250, 1000, 1000, 12500, 1250, 1250, 1250, 1000, 12500, 12500, 1000, 1250, 12500, 1250])], axis=1)
        tbl_0 = 0.05 * jax.random.normal(jax.random.fold_in(_tk, 500 + 0), (1000, 16), jnp.float32)
        tbl_1 = 0.05 * jax.random.normal(jax.random.fold_in(_tk, 500 + 1), (1250, 16), jnp.float32)
        tbl_2 = 0.05 * jax.random.normal(jax.random.fold_in(_tk, 500 + 2), (1000, 16), jnp.float32)
        tbl_3 = 0.05 * jax.random.normal(jax.random.fold_in(_tk, 500 + 3), (1250, 16), jnp.float32)
        tbl_4 = 0.05 * jax.random.normal(jax.random.fold_in(_tk, 500 + 4), (12500, 16), jnp.float32)
        tbl_5 = 0.05 * jax.random.normal(jax.random.fold_in(_tk, 500 + 5), (1250, 16), jnp.float32)
        tbl_6 = 0.05 * jax.random.normal(jax.random.fold_in(_tk, 500 + 6), (1250, 16), jnp.float32)
        tbl_7 = 0.05 * jax.random.normal(jax.random.fold_in(_tk, 500 + 7), (12500, 16), jnp.float32)
        tbl_8 = 0.05 * jax.random.normal(jax.random.fold_in(_tk, 500 + 8), (1250, 16), jnp.float32)
        tbl_9 = 0.05 * jax.random.normal(jax.random.fold_in(_tk, 500 + 9), (125000, 16), jnp.float32)
        tbl_10 = 0.05 * jax.random.normal(jax.random.fold_in(_tk, 500 + 10), (125000, 16), jnp.float32)
        tbl_11 = 0.05 * jax.random.normal(jax.random.fold_in(_tk, 500 + 11), (125000, 16), jnp.float32)
        tbl_12 = 0.05 * jax.random.normal(jax.random.fold_in(_tk, 500 + 12), (1000, 16), jnp.float32)
        tbl_13 = 0.05 * jax.random.normal(jax.random.fold_in(_tk, 500 + 13), (125000, 16), jnp.float32)
        tbl_14 = 0.05 * jax.random.normal(jax.random.fold_in(_tk, 500 + 14), (1000, 16), jnp.float32)
        tbl_15 = 0.05 * jax.random.normal(jax.random.fold_in(_tk, 500 + 15), (1250, 16), jnp.float32)
        tbl_16 = 0.05 * jax.random.normal(jax.random.fold_in(_tk, 500 + 16), (1000, 16), jnp.float32)
        tbl_17 = 0.05 * jax.random.normal(jax.random.fold_in(_tk, 500 + 17), (1250, 16), jnp.float32)
        tbl_18 = 0.05 * jax.random.normal(jax.random.fold_in(_tk, 500 + 18), (1250, 16), jnp.float32)
        tbl_19 = 0.05 * jax.random.normal(jax.random.fold_in(_tk, 500 + 19), (125000, 16), jnp.float32)
        tbl_20 = 0.05 * jax.random.normal(jax.random.fold_in(_tk, 500 + 20), (1000, 16), jnp.float32)
        tbl_21 = 0.05 * jax.random.normal(jax.random.fold_in(_tk, 500 + 21), (125000, 16), jnp.float32)
        tbl_22 = 0.05 * jax.random.normal(jax.random.fold_in(_tk, 500 + 22), (1250, 16), jnp.float32)
        tbl_23 = 0.05 * jax.random.normal(jax.random.fold_in(_tk, 500 + 23), (1000, 16), jnp.float32)
        tbl_24 = 0.05 * jax.random.normal(jax.random.fold_in(_tk, 500 + 24), (125000, 16), jnp.float32)
        tbl_25 = 0.05 * jax.random.normal(jax.random.fold_in(_tk, 500 + 25), (1250, 16), jnp.float32)
        tbl_26 = 0.05 * jax.random.normal(jax.random.fold_in(_tk, 500 + 26), (1000, 16), jnp.float32)
        tbl_27 = 0.05 * jax.random.normal(jax.random.fold_in(_tk, 500 + 27), (1000, 16), jnp.float32)
        tbl_28 = 0.05 * jax.random.normal(jax.random.fold_in(_tk, 500 + 28), (12500, 16), jnp.float32)
        tbl_29 = 0.05 * jax.random.normal(jax.random.fold_in(_tk, 500 + 29), (1250, 16), jnp.float32)
        tbl_30 = 0.05 * jax.random.normal(jax.random.fold_in(_tk, 500 + 30), (1250, 16), jnp.float32)
        tbl_31 = 0.05 * jax.random.normal(jax.random.fold_in(_tk, 500 + 31), (1250, 16), jnp.float32)
        tbl_32 = 0.05 * jax.random.normal(jax.random.fold_in(_tk, 500 + 32), (1000, 16), jnp.float32)
        tbl_33 = 0.05 * jax.random.normal(jax.random.fold_in(_tk, 500 + 33), (12500, 16), jnp.float32)
        tbl_34 = 0.05 * jax.random.normal(jax.random.fold_in(_tk, 500 + 34), (12500, 16), jnp.float32)
        tbl_35 = 0.05 * jax.random.normal(jax.random.fold_in(_tk, 500 + 35), (1000, 16), jnp.float32)
        tbl_36 = 0.05 * jax.random.normal(jax.random.fold_in(_tk, 500 + 36), (1250, 16), jnp.float32)
        tbl_37 = 0.05 * jax.random.normal(jax.random.fold_in(_tk, 500 + 37), (12500, 16), jnp.float32)
        tbl_38 = 0.05 * jax.random.normal(jax.random.fold_in(_tk, 500 + 38), (1250, 16), jnp.float32)
        _rk = jax.random.fold_in(_tk, 7)
        W_top1 = 0.0693375 * jax.random.normal(jax.random.fold_in(_tk, 801), (208, 512), jnp.float32)
        W_top2 = 0.0441942 * jax.random.normal(jax.random.fold_in(_tk, 802), (512, 256), jnp.float32)
        W_top3 = 0.0625 * jax.random.normal(jax.random.fold_in(_tk, 803), (256, 1), jnp.float32)
        b_top1 = jnp.zeros((512,), jnp.float32)
        b_top2 = jnp.zeros((256,), jnp.float32)
        return (dense_ctx, ids, tbl_0, tbl_1, tbl_2, tbl_3, tbl_4, tbl_5, tbl_6, tbl_7, tbl_8, tbl_9, tbl_10, tbl_11, tbl_12, tbl_13, tbl_14, tbl_15, tbl_16, tbl_17, tbl_18, tbl_19, tbl_20, tbl_21, tbl_22, tbl_23, tbl_24, tbl_25, tbl_26, tbl_27, tbl_28, tbl_29, tbl_30, tbl_31, tbl_32, tbl_33, tbl_34, tbl_35, tbl_36, tbl_37, tbl_38, W_top1, b_top1, W_top2, b_top2, W_top3)
    dense_ctx, ids, tbl_0, tbl_1, tbl_2, tbl_3, tbl_4, tbl_5, tbl_6, tbl_7, tbl_8, tbl_9, tbl_10, tbl_11, tbl_12, tbl_13, tbl_14, tbl_15, tbl_16, tbl_17, tbl_18, tbl_19, tbl_20, tbl_21, tbl_22, tbl_23, tbl_24, tbl_25, tbl_26, tbl_27, tbl_28, tbl_29, tbl_30, tbl_31, tbl_32, tbl_33, tbl_34, tbl_35, tbl_36, tbl_37, tbl_38, W_top1, b_top1, W_top2, b_top2, W_top3 = _rec_inputs()

    def _L0_rec_setup():
        import jax, jax.numpy as jnp
        import numpy as np
        key = jax.random.key(seed)
        k1, k2, k3 = jax.random.split(key, 3)
        B, F0, D = (1024, 39, 16)
        L = 128
        hash_x = jax.random.normal(k1, (B, F0, D), dtype=jnp.float32)
        W0 = jax.random.normal(k2, (F0 * F0, L), dtype=jnp.float32) * 0.05
        W1 = jax.random.normal(k3, (F0 * (L // 2), L), dtype=jnp.float32) * 0.05
        return {'hash_x': hash_x, 'W0': W0, 'W1': W1}
    _L0_rec_all = _L0_rec_setup()
    _L0_rec_in = {k: v for k, v in _L0_rec_all.items() if k in ('W0', 'W1')}
    del _L0_rec_all
    return {'dense_ctx': dense_ctx, 'ids': ids, 'tbl_0': tbl_0, 'tbl_1': tbl_1, 'tbl_2': tbl_2, 'tbl_3': tbl_3, 'tbl_4': tbl_4, 'tbl_5': tbl_5, 'tbl_6': tbl_6, 'tbl_7': tbl_7, 'tbl_8': tbl_8, 'tbl_9': tbl_9, 'tbl_10': tbl_10, 'tbl_11': tbl_11, 'tbl_12': tbl_12, 'tbl_13': tbl_13, 'tbl_14': tbl_14, 'tbl_15': tbl_15, 'tbl_16': tbl_16, 'tbl_17': tbl_17, 'tbl_18': tbl_18, 'tbl_19': tbl_19, 'tbl_20': tbl_20, 'tbl_21': tbl_21, 'tbl_22': tbl_22, 'tbl_23': tbl_23, 'tbl_24': tbl_24, 'tbl_25': tbl_25, 'tbl_26': tbl_26, 'tbl_27': tbl_27, 'tbl_28': tbl_28, 'tbl_29': tbl_29, 'tbl_30': tbl_30, 'tbl_31': tbl_31, 'tbl_32': tbl_32, 'tbl_33': tbl_33, 'tbl_34': tbl_34, 'tbl_35': tbl_35, 'tbl_36': tbl_36, 'tbl_37': tbl_37, 'tbl_38': tbl_38, 'W_top1': W_top1, 'b_top1': b_top1, 'W_top2': W_top2, 'b_top2': b_top2, 'W_top3': W_top3, 'L0_rec_W0': _L0_rec_in['W0'], 'L0_rec_W1': _L0_rec_in['W1']}

def reference(dense_ctx, ids, tbl_0, tbl_1, tbl_2, tbl_3, tbl_4, tbl_5, tbl_6, tbl_7, tbl_8, tbl_9, tbl_10, tbl_11, tbl_12, tbl_13, tbl_14, tbl_15, tbl_16, tbl_17, tbl_18, tbl_19, tbl_20, tbl_21, tbl_22, tbl_23, tbl_24, tbl_25, tbl_26, tbl_27, tbl_28, tbl_29, tbl_30, tbl_31, tbl_32, tbl_33, tbl_34, tbl_35, tbl_36, tbl_37, tbl_38, W_top1, b_top1, W_top2, b_top2, W_top3, L0_rec_W0, L0_rec_W1):
    import jax
    import jax.numpy as jnp

    def _L0_rec_ref(hash_x, W0, W1):
        import jax, jax.numpy as jnp
        import numpy as np
        x0 = hash_x
        B, F0, D = x0.shape
        L = W0.shape[1]
        z0 = jnp.einsum('bid,bjd->bdij', x0, x0).reshape(B, D, F0 * F0)
        cur0 = jax.nn.relu(jnp.einsum('bdk,kl->bld', z0, W0))
        next_h, direct0 = jnp.split(cur0, 2, axis=1)
        Fk = next_h.shape[1]
        z1 = jnp.einsum('bid,bjd->bdij', x0, next_h).reshape(B, D, F0 * Fk)
        cur1 = jax.nn.relu(jnp.einsum('bdk,kl->bld', z1, W1))
        result = jnp.concatenate([direct0, cur1], axis=1)
        return jnp.sum(result, axis=-1)
    e = jnp.stack([tbl_0[ids[:, 0]], tbl_1[ids[:, 1]], tbl_2[ids[:, 2]], tbl_3[ids[:, 3]], tbl_4[ids[:, 4]], tbl_5[ids[:, 5]], tbl_6[ids[:, 6]], tbl_7[ids[:, 7]], tbl_8[ids[:, 8]], tbl_9[ids[:, 9]], tbl_10[ids[:, 10]], tbl_11[ids[:, 11]], tbl_12[ids[:, 12]], tbl_13[ids[:, 13]], tbl_14[ids[:, 14]], tbl_15[ids[:, 15]], tbl_16[ids[:, 16]], tbl_17[ids[:, 17]], tbl_18[ids[:, 18]], tbl_19[ids[:, 19]], tbl_20[ids[:, 20]], tbl_21[ids[:, 21]], tbl_22[ids[:, 22]], tbl_23[ids[:, 23]], tbl_24[ids[:, 24]], tbl_25[ids[:, 25]], tbl_26[ids[:, 26]], tbl_27[ids[:, 27]], tbl_28[ids[:, 28]], tbl_29[ids[:, 29]], tbl_30[ids[:, 30]], tbl_31[ids[:, 31]], tbl_32[ids[:, 32]], tbl_33[ids[:, 33]], tbl_34[ids[:, 34]], tbl_35[ids[:, 35]], tbl_36[ids[:, 36]], tbl_37[ids[:, 37]], tbl_38[ids[:, 38]]], axis=1)
    z = _L0_rec_ref(e, L0_rec_W0, L0_rec_W1)
    z = z.reshape(z.shape[0], -1)
    h = jnp.concatenate([z, dense_ctx], axis=1)
    h = jnp.maximum(h @ W_top1 + b_top1, 0.0)
    h = jnp.maximum(h @ W_top2 + b_top2, 0.0)
    y = h @ W_top3
    return y

_drawn_inputs = setup_inputs


def setup_inputs(seed=0):
    import zlib

    import numpy as np

    out = dict(_drawn_inputs(seed))
    spreads = {'b_top1': (0.0, 0.8), 'b_top2': (0.0, 0.448)}
    factors = {'tbl_0': 8.0,
     'tbl_1': 8.0,
     'tbl_2': 8.0,
     'tbl_3': 8.0,
     'tbl_4': 8.0,
     'tbl_5': 8.0,
     'tbl_6': 8.0,
     'tbl_7': 8.0,
     'tbl_8': 8.0,
     'tbl_9': 8.0,
     'tbl_10': 8.0,
     'tbl_11': 8.0,
     'tbl_12': 8.0,
     'tbl_13': 8.0,
     'tbl_14': 8.0,
     'tbl_15': 8.0,
     'tbl_16': 8.0,
     'tbl_17': 8.0,
     'tbl_18': 8.0,
     'tbl_19': 8.0,
     'tbl_20': 8.0,
     'tbl_21': 8.0,
     'tbl_22': 8.0,
     'tbl_23': 8.0,
     'tbl_24': 8.0,
     'tbl_25': 8.0,
     'tbl_26': 8.0,
     'tbl_27': 8.0,
     'tbl_28': 8.0,
     'tbl_29': 8.0,
     'tbl_30': 8.0,
     'tbl_31': 8.0,
     'tbl_32': 8.0,
     'tbl_33': 8.0,
     'tbl_34': 8.0,
     'tbl_35': 8.0,
     'tbl_36': 8.0,
     'tbl_37': 8.0,
     'tbl_38': 8.0,
     'L0_rec_W1': 8.0}
    for name, (base, spread) in spreads.items():
        noise = np.random.default_rng([zlib.crc32(name.encode()), seed]).standard_normal(out[name].shape)
        drawn = base * np.exp(spread * noise) if base else spread * noise
        out[name] = jnp.asarray(drawn.astype(out[name].dtype))
    for name, factor in factors.items():
        out[name] = (out[name] * factor).astype(out[name].dtype)
    return out
```

```python
import concourse.bass as bass
from concourse import mybir
from contextlib import ExitStack

F = 39
D = 16
B = 1024
P = 128
NBLK = B // P
DC = 4
NCH = D // DC
CH = DC * P
L = 128
HK = L // 2
PARTS = 3
FP = PARTS * F
NSHIFT = (F + 1) // 2
T0 = -(-NSHIFT // 3)
LAST0 = (NSHIFT - 3 * (T0 - 1)) * F
T1 = -(-F // 2)
PAIR0 = -(-T0 // 2)
PAIR1 = T1 // 2
PAIRS = PAIR0 + PAIR1
ZS = 4
M1, M2 = 512, 256
NCTX = 16


def dlrm_tower(nc, A, y_out):
    fp32, bf16, i32, u32 = mybir.dt.float32, mybir.dt.bfloat16, mybir.dt.int32, mybir.dt.uint32
    ALU = mybir.AluOpType
    ACT = mybir.ActivationFunctionType
    AX = mybir.AxisListType

    ctx = ExitStack()
    with ctx:
        def sb(name, shape, dt):
            return ctx.enter_context(nc.sbuf_tensor(name, shape, dt))

        def ps(name, shape, dt):
            return ctx.enter_context(nc.psum_tensor(name, shape, dt))

        def sem(name):
            return ctx.enter_context(nc.semaphore(name))

        ids_all = sb("ids_all", [P, NBLK, F], i32)
        ids_now = sb("ids_now", [P, F], i32)
        emb = sb("emb", [P, F * D], fp32)
        rest = sb("rest", [P, F, D], fp32)
        parts = sb("parts", [P, D, PARTS, F], bf16)
        spread1 = sb("spread1", [FP, T1, L], bf16)
        shift0 = sb("shift0", [FP, T0, FP], bf16)
        repeat0 = sb("repeat0", [FP, FP], bf16)
        ident = sb("ident", [P, P], bf16)
        w0_ij = sb("w0_ij", [FP, T0, L], fp32)
        w0_ji = sb("w0_ji", [FP, T0, L], fp32)
        w0 = sb("w0", [FP, T0, L], fp32)
        w1 = sb("w1", [P, T1, L], fp32)
        xparts = sb("xparts", [FP, NCH, CH], bf16)
        x3 = sb("x3", [FP, NCH, CH], fp32)
        h2 = sb("h2", [P, 2, CH], fp32)
        z = sb("z", [P, ZS, 2, CH], fp32)
        sum_d = sb("sum_d", [HK, DC, P], fp32)
        sum_c = sb("sum_c", [L, DC, P], fp32)
        feat_a = sb("feat_a", [HK + NCTX, B], fp32)
        feat_b = sb("feat_b", [L, B], fp32)
        wt1a = sb("wt1a", [HK + NCTX, M1], fp32)
        wt1b = sb("wt1b", [L, M1], fp32)
        wt2 = sb("wt2", [P, M1 // P, M2], fp32)
        wt3 = sb("wt3", [P, M2 // P], fp32)
        b1 = sb("b1", [P, M1 // P], fp32)
        b2 = sb("b2", [P, M2 // P], fp32)
        hid1 = sb("hid1", [P, M1 // P, CH], fp32)
        hid2 = sb("hid2", [P, M2 // P, CH], fp32)
        y_row = sb("y_row", [1, B], fp32)

        xb = [ps(f"xb{n}", [P, 2, CH], fp32) for n in range(2)]
        out0 = ps("out0", [P, CH], fp32)
        out1 = ps("out1", [P, CH], fp32)
        t_ps = ps("t_ps", [P, 2 * CH], bf16)
        x3_ps = ps("x3_ps", [P, CH], fp32)

        ids_in = sem("ids_in")
        consts_in = sem("consts_in")
        w0_in = sem("w0_in")
        w0_ready = sem("w0_ready")
        w1_in = sem("w1_in")
        top_in = sem("top_in")
        ids_copied = sem("ids_copied")
        gathered = sem("gathered")
        pool_turns = sem("pool_turns")
        split_step = sem("split_step")
        transposed = sem("transposed")
        xparts_ready = sem("xparts_ready")
        x3_made = sem("x3_made")
        x3_ready = sem("x3_ready")
        spread_done = sem("spread_done")
        prod_done = sem("prod_done")
        pair_used = sem("pair_used")
        h2_ready = sem("h2_ready")
        direct_done = sem("direct_done")
        cur1_done = sem("cur1_done")
        feat_ready = sem("feat_ready")
        mlp1_done = sem("mlp1_done")
        hid1_ready = sem("hid1_ready")
        mlp2_done = sem("mlp2_done")
        hid2_ready = sem("hid2_ready")
        mlp3_done = sem("mlp3_done")
        y_ready = sem("y_ready")
        y_out_done = sem("y_out_done")

        block = ctx.enter_context(nc.Block())

        def step_pairs(c, final):
            l0 = [] if final else [(0, (c + 1) % NCH, k) for k in range(PAIR0)]
            return l0 + [(1, c, k) for k in range(PAIR1)]

        def following(c, last):
            if last and c == NCH - 1:
                return []
            return step_pairs((c + 1) % NCH, last and c + 1 == NCH - 1)[:2]

        def pair_number(blk, c, pos):
            return blk * (NCH * PAIRS) + (PAIR0 + c * PAIRS + pos)

        def slot_of(c, pos, n):
            return (PAIR0 + c * PAIRS + pos) % n

        def tiles_of(layer, k):
            count = T0 if layer == 0 else T1
            return [t for t in (2 * k, 2 * k + 1) if t < count]

        @block.sync
        def _(sp):
            sp.dma_start(ids_all[:], A["ids"].rearrange("(n p) f -> p n f", p=P)).then_inc(ids_in, 16)
            sp.dma_start(ident[:], A["ident"]).then_inc(consts_in, 16)
            sp.dma_start(repeat0[:], A["repeat0"]).then_inc(consts_in, 16)
            sp.dma_start(shift0[:], A["shift0"].rearrange("p (t m) -> p t m", t=T0)).then_inc(consts_in, 16)
            sp.dma_start(spread1[:], A["spread1"].rearrange("p (t m) -> p t m", t=T1)).then_inc(consts_in, 16)
            full = (T0 - 1) * FP
            for src, dst in ((A["w0_ij"], w0_ij), (A["w0_ji"], w0_ji)):
                sp.dma_start(dst[:, 0:T0 - 1, :],
                             src[0:full, :].rearrange("(t p) l -> p t l", p=FP)).then_inc(w0_in, 16)
                sp.dma_start(dst[0:LAST0, T0 - 1, :], src[full:full + LAST0, :]).then_inc(w0_in, 16)
            full = (T1 - 1) * P
            sp.dma_start(w1[:, 0:T1 - 1, :],
                         A["W1"][0:full, :].rearrange("(t p) l -> p t l", p=P)).then_inc(w1_in, 16)
            sp.dma_start(w1[0:HK, T1 - 1, :], A["W1"][full:full + HK, :]).then_inc(w1_in, 16)
            sp.dma_start(wt1a[0:HK, :], A["W_top1"][0:HK, :]).then_inc(top_in, 16)
            sp.dma_start(wt1a[HK:HK + NCTX, :], A["W_top1"][HK + L:HK + L + NCTX, :]).then_inc(top_in, 16)
            sp.dma_start(wt1b[:], A["W_top1"][HK:HK + L, :]).then_inc(top_in, 16)
            sp.dma_start(wt2[:], A["W_top2"].rearrange("(k p) n -> p k n", p=P)).then_inc(top_in, 16)
            sp.dma_start(wt3[:], A["W_top3"]).then_inc(top_in, 16)
            sp.dma_start(b1[:], A["b_top1"]).then_inc(top_in, 16)
            sp.dma_start(b2[:], A["b_top2"]).then_inc(top_in, 16)
            sp.dma_start(feat_a[HK:HK + NCTX, :], A["dense_ctx"]).then_inc(top_in, 16)
            sp.wait_ge(y_ready, 2)
            sp.dma_start(y_out.rearrange("b o -> o b"), y_row[:]).then_inc(y_out_done, 16)
            sp.wait_ge(y_out_done, 16)

        @block.gpsimd
        def _(pool):
            embv = emb[:].rearrange("p (f d) -> p f d", f=F)

            def part(n):
                return parts[:, :, n, :].rearrange("p d f -> p f d")

            def stand_alone():
                pool.sem_inc(pool_turns, 1)

            pool.wait_ge(ids_in, 16)
            with pool.Fori(0, NBLK) as blk:
                nc.gpsimd.tensor_copy(ids_now[:], ids_all[:, bass.ds(blk, 1), :].rearrange(
                    "p o f -> p (o f)")).then_inc(ids_copied, 1)
                pool.wait_ge(ids_copied, blk + 1)
                stand_alone()
                for f in range(F):
                    nc.gpsimd.indirect_dma_start(
                        out=emb[:, f * D:(f + 1) * D], out_offset=None, in_=A[f"tbl_{f}"],
                        in_offset=bass.IndirectOffsetOnAxis(ap=ids_now[:, f:f + 1].bitcast(u32), axis=0),
                    ).then_inc(gathered, 16)
                pool.wait_ge(gathered, blk * (16 * F) + 16 * F)
                pool.wait_ge(transposed, blk * NCH + 1)
                stand_alone()
                nc.gpsimd.tensor_copy(part(0), embv).then_inc(split_step, 1)
                pool.wait_ge(split_step, blk * 4 + 1)
                nc.gpsimd.tensor_tensor(rest[:], embv, part(0), ALU.subtract).then_inc(split_step, 1)
                pool.wait_ge(split_step, blk * 4 + 2)
                stand_alone()
                nc.gpsimd.tensor_copy(part(1), rest[:]).then_inc(split_step, 1)
                pool.wait_ge(split_step, blk * 4 + 3)
                nc.gpsimd.tensor_tensor(part(2), rest[:], part(1), ALU.subtract).then_inc(split_step, 1)
                pool.wait_ge(split_step, blk * 4 + 4)
                stand_alone()

        @block.tensor
        def _(pe):
            def transpose_chunk(chunk_no, block_no, c):
                pe.wait_ge(split_step, block_no * 4 + 4)
                pe.wait_ge(xparts_ready, chunk_no)
                for q in range(DC):
                    last = nc.tensor.transpose(
                        t_ps[0:FP, q * P:(q + 1) * P],
                        parts[:, c * DC + q, :, :].rearrange("p a f -> p (a f)"), ident[:])
                last.then_inc(transposed, 1)

            def make_x3(chunk_no, c):
                pe.wait_ge(xparts_ready, chunk_no + 1)
                pe.wait_ge(x3_ready, chunk_no)
                nc.tensor.matmul(x3_ps[0:FP, :], repeat0[:], xparts[:, c, :],
                                 start=True, stop=True).then_inc(x3_made, 1)

            def spread(pair, slot):
                layer, c, k = pair
                for n, t in enumerate(tiles_of(layer, k)):
                    if layer == 0:
                        last = nc.tensor.matmul(xb[slot][0:FP, n, :], shift0[:, t, :], xparts[:, c, :],
                                                start=True, stop=True)
                    else:
                        last = nc.tensor.matmul(xb[slot][:, n, :], spread1[:, t, :], xparts[:, c, :],
                                                start=True, stop=True)
                last.then_inc(spread_done, 1)

            def contract(pair, slot, l0_chunk, l1_chunk):
                layer, c, k = pair
                if layer == 0 and k == 0:
                    pe.wait_ge(h2_ready, l0_chunk * 2)
                    pe.wait_ge(direct_done, l0_chunk)
                if layer == 1 and k == 0:
                    pe.wait_ge(cur1_done, l1_chunk + 1)
                for n, t in enumerate(tiles_of(layer, k)):
                    if layer == 0:
                        rows = FP if t < T0 - 1 else LAST0
                        last = nc.tensor.matmul(out0[:], w0[0:rows, t, :], z[0:rows, slot, n, :],
                                                start=(t == 0), stop=(t == T0 - 1))
                    else:
                        rows = P if t < T1 - 1 else HK
                        last = nc.tensor.matmul(out1[:], w1[0:rows, t, :], z[0:rows, slot, n, :],
                                                start=(t == 0), stop=(t == T1 - 1))
                last.then_inc(pair_used, 1)

            def step(blk, c, last):
                final = last and c == NCH - 1
                pairs = step_pairs(c, final)
                ahead = pairs + following(c, last)
                for pos, pair in enumerate(pairs):
                    pe.wait_ge(prod_done, pair_number(blk, c, pos) + 1)
                    if pos + 2 < len(ahead):
                        spread(ahead[pos + 2], slot_of(c, pos, 2))
                    contract(pair, slot_of(c, pos, ZS), blk * NCH + (c + 1), blk * NCH + c)
                    if pos == PAIR0 and c > 0 and not last:
                        make_x3(blk * NCH + (c - 1 + NCH), c - 1)
                    if pos == PAIR0 and c == 0:
                        make_x3(blk * NCH + (NCH - 1), NCH - 1)
                if not last:
                    transpose_chunk(blk * NCH + (c + NCH), blk + 1, c)

            pe.sem_inc(transposed, 1)
            pe.wait_ge(consts_in, 64)
            for c in range(NCH):
                transpose_chunk(c, 0, c)
                if c > 0:
                    make_x3(c - 1, c - 1)
            opening = [(0, 0, k) for k in range(PAIR0)] + step_pairs(0, False)[:2]
            spread(opening[0], 0)
            spread(opening[1], 1)
            pe.wait_ge(w0_ready, 2)
            for k in range(PAIR0):
                pe.wait_ge(prod_done, k + 1)
                spread(opening[k + 2], k % 2)
                for n, t in enumerate(tiles_of(0, k)):
                    rows = FP if t < T0 - 1 else LAST0
                    end = nc.tensor.matmul(out0[:], w0[0:rows, t, :], z[0:rows, k % ZS, n, :],
                                           start=(t == 0), stop=(t == T0 - 1))
                end.then_inc(pair_used, 1)
            pe.wait_ge(w1_in, 32)
            with pe.Fori(0, NBLK - 1) as blk:
                for c in range(NCH):
                    step(blk, c, False)
            for c in range(NCH):
                step(NBLK - 1, c, True)

            pe.wait_ge(top_in, 128)
            pe.wait_ge(feat_ready, 2 * NBLK)
            n1, n2 = M1 // P, M2 // P
            for half in range(B // CH):
                cols = slice(half * CH, (half + 1) * CH)
                for m in range(n1):
                    if half:
                        pe.wait_ge(hid1_ready, m + 1)
                    dst = xb[m // 2][:, m % 2, :]
                    nc.tensor.matmul(dst, wt1a[:, m * P:(m + 1) * P], feat_a[:, cols], start=True, stop=False)
                    nc.tensor.matmul(dst, wt1b[:, m * P:(m + 1) * P], feat_b[:, cols],
                                     start=False, stop=True).then_inc(mlp1_done, 1)
                pe.wait_ge(hid1_ready, n1 * (half + 1))
                for m in range(n2):
                    if half:
                        pe.wait_ge(hid2_ready, m + 1)
                    dst = (out0, out1)[m]
                    for k in range(n1):
                        last = nc.tensor.matmul(dst[:], wt2[:, k, m * P:(m + 1) * P], hid1[:, k, :],
                                                start=(k == 0), stop=(k == n1 - 1))
                    last.then_inc(mlp2_done, 1)
                pe.wait_ge(hid2_ready, n2 * (half + 1))
                if half:
                    pe.wait_ge(y_ready, half)
                for k in range(n2):
                    last = nc.tensor.matmul(x3_ps[0:1, :], wt3[:, k:k + 1], hid2[:, k, :],
                                            start=(k == 0), stop=(k == n2 - 1))
                last.then_inc(mlp3_done, 1)

        @block.scalar
        def _(act):
            def copy_xparts(chunk_no, c):
                act.wait_ge(transposed, chunk_no + 2)
                nc.scalar.copy(xparts[:, c, :], t_ps[0:FP, 0:CH]).then_inc(xparts_ready, 1)

            def copy_x3(chunk_no, c):
                act.wait_ge(x3_made, chunk_no + 1)
                nc.scalar.copy(x3[:, c, :], x3_ps[0:FP, :]).then_inc(x3_ready, 1)

            def relu_next(pairs_used, slot):
                act.wait_ge(pair_used, pairs_used)
                for half in range(2):
                    nc.scalar.activation(h2[half * HK:(half + 1) * HK, slot, :], out0[HK:L, :],
                                         ACT.Relu).then_inc(h2_ready, 1)

            def step(blk, c, last):
                if not (last and c == NCH - 1):
                    relu_next(pair_number(blk, c, PAIR0), (c + 1) % 2)
                if c == 0:
                    copy_x3(blk * NCH + (NCH - 1), NCH - 1)
                elif not last:
                    copy_x3(blk * NCH + (c - 1 + NCH), c - 1)
                if not last:
                    copy_xparts(blk * NCH + (c + NCH), c)

            for c in range(NCH):
                copy_xparts(c, c)
                if c > 0:
                    copy_x3(c - 1, c - 1)
            relu_next(PAIR0, 0)
            with act.Fori(0, NBLK - 1) as blk:
                for c in range(NCH):
                    step(blk, c, False)
            for c in range(NCH):
                step(NBLK - 1, c, True)

            n1, n2 = M1 // P, M2 // P
            act.wait_ge(top_in, 128)
            for half in range(B // CH):
                for m in range(n1):
                    act.wait_ge(mlp1_done, half * n1 + m + 1)
                    if half:
                        act.wait_ge(mlp2_done, n2)
                    nc.scalar.activation(hid1[:, m, :], xb[m // 2][:, m % 2, :], ACT.Relu,
                                         bias=b1[:, m:m + 1]).then_inc(hid1_ready, 1)
                for m in range(n2):
                    act.wait_ge(mlp2_done, half * n2 + m + 1)
                    if half:
                        act.wait_ge(mlp3_done, 1)
                    nc.scalar.activation(hid2[:, m, :], (out0, out1)[m][:], ACT.Relu,
                                         bias=b2[:, m:m + 1]).then_inc(hid2_ready, 1)
                act.wait_ge(mlp3_done, half + 1)
                nc.scalar.copy(y_row[0:1, half * CH:(half + 1) * CH], x3_ps[0:1, :]).then_inc(y_ready, 1)

        @block.vector
        def _(dve):
            dve.sem_inc(cur1_done, 1)
            dve.wait_ge(w0_in, 64)
            for half in range(2):
                to, frm = slice(half * HK, (half + 1) * HK), slice((1 - half) * HK, (2 - half) * HK)
                nc.vector.tensor_tensor(w0[:, 0:T0 - 1, to], w0_ij[:, 0:T0 - 1, frm],
                                        w0_ji[:, 0:T0 - 1, frm], ALU.add)
                last = nc.vector.tensor_tensor(w0[0:LAST0, T0 - 1, to], w0_ij[0:LAST0, T0 - 1, frm],
                                               w0_ji[0:LAST0, T0 - 1, frm], ALU.add)
                last.then_inc(w0_ready, 1)

            def product(pair, number, zslot, xslot, l0_chunk, l1_chunk, free):
                layer, c, k = pair
                if layer == 0 and k == 0:
                    dve.wait_ge(x3_ready, l0_chunk + 1)
                if layer == 1 and k == 0:
                    dve.wait_ge(h2_ready, l1_chunk * 2 + 2)
                dve.wait_ge(spread_done, number + 1)
                if free:
                    dve.wait_ge(pair_used, number - (ZS - 1))
                n = len(tiles_of(layer, k))
                rows = FP if layer == 0 else P
                fixed = x3[:, c, :] if layer == 0 else h2[:, c % 2, :]
                nc.vector.tensor_tensor(z[0:rows, zslot, 0:n, :], xb[xslot][0:rows, 0:n, :],
                                        fixed.unsqueeze(1).to_broadcast([rows, n, CH]),
                                        ALU.mult).then_inc(prod_done, 1)

            def add_direct(blk, chunk_no, c, pairs_used):
                dve.wait_ge(pair_used, pairs_used)
                flat = sum_d[:].rearrange("l q b -> l (q b)")
                if c == 0:
                    nc.vector.tensor_scalar(flat, out0[0:HK, :], 0.0, None, ALU.max).then_inc(direct_done, 1)
                else:
                    dve.wait_ge(direct_done, chunk_no)
                    nc.vector.scalar_tensor_tensor(flat, out0[0:HK, :], 0.0, flat,
                                                   ALU.max, ALU.add).then_inc(direct_done, 1)
                if c == NCH - 1:
                    dve.wait_ge(direct_done, chunk_no + 1)
                    nc.vector.tensor_reduce(feat_a[0:HK, bass.ds(blk * P, P)],
                                            sum_d[:].rearrange("l q b -> l b q"),
                                            AX.X, ALU.add).then_inc(feat_ready, 1)

            def add_cur1(blk, chunk_no, c, pairs_used):
                dve.wait_ge(pair_used, pairs_used)
                flat = sum_c[:].rearrange("l q b -> l (q b)")
                if c == 0:
                    nc.vector.tensor_scalar(flat, out1[:], 0.0, None, ALU.max).then_inc(cur1_done, 1)
                else:
                    dve.wait_ge(cur1_done, chunk_no + 1)
                    nc.vector.scalar_tensor_tensor(flat, out1[:], 0.0, flat,
                                                   ALU.max, ALU.add).then_inc(cur1_done, 1)
                if c == NCH - 1:
                    dve.wait_ge(cur1_done, chunk_no + 2)
                    nc.vector.tensor_reduce(feat_b[:, bass.ds(blk * P, P)],
                                            sum_c[:].rearrange("l q b -> l b q"),
                                            AX.X, ALU.add).then_inc(feat_ready, 1)

            def step(blk, c, last):
                final = last and c == NCH - 1
                pairs = step_pairs(c, final)
                ahead = pairs + following(c, last)
                for pos in range(2, len(ahead)):
                    chunk = blk * NCH + c
                    nxt = pos >= len(pairs)
                    l0_chunk = chunk + (2 if nxt else 1)
                    l1_chunk = chunk + (1 if nxt else 0)
                    product(ahead[pos], pair_number(blk, c, pos), slot_of(c, pos, ZS),
                            slot_of(c, pos, 2), l0_chunk, l1_chunk, True)
                    if pos == PAIR0 + 2 and not final:
                        add_direct(blk if c < NCH - 1 else blk + 1, chunk + 1, (c + 1) % NCH,
                                   pair_number(blk, c, PAIR0))
                add_cur1(blk, blk * NCH + c, c, pair_number(blk, c, len(pairs)))

            opening = [(0, 0, k) for k in range(PAIR0)] + step_pairs(0, False)[:2]
            for n, pair in enumerate(opening):
                product(pair, n, n % ZS, n % 2, 0 if n < PAIR0 else 1, 0, n >= ZS)
                if n == PAIR0 + 1:
                    add_direct(0, 0, 0, PAIR0)
            with dve.Fori(0, NBLK - 1) as blk:
                for c in range(NCH):
                    step(blk, c, False)
            for c in range(NCH):
                step(NBLK - 1, c, True)


def kernel(**inputs):
    import numpy as np
    import ml_dtypes
    import concourse.bacc as bacc
    from concourse import mybir as mb
    from concourse.bass_utils import run_bass_kernel_spmd as run

    def c(a):
        return np.ascontiguousarray(np.asarray(a))

    field = np.arange(FP) % F
    col_i, col_s = np.arange(FP) % F, np.arange(FP) // F
    one = ml_dtypes.bfloat16
    shift0 = np.stack([field[:, None] == (col_i + 3 * t + col_s)[None, :] % F for t in range(T0)], 1)
    spread1 = np.stack([field[:, None] == (2 * t + np.arange(L) // HK).clip(max=F - 1)[None, :]
                        for t in range(T1)], 1)
    s, i = np.meshgrid(np.arange(NSHIFT), np.arange(F), indexing="ij")
    j = (i + s) % F
    W0 = c(inputs["L0_rec_W0"])
    w0_ji = W0[(j * F + i).ravel()[F:]]

    arrays = {
        "ids": c(inputs["ids"]),
        "ident": np.eye(P, dtype=one),
        "repeat0": (field[:, None] == col_i[None, :]).astype(one),
        "shift0": shift0.reshape(FP, T0 * FP).astype(one),
        "spread1": spread1.reshape(FP, T1 * L).astype(one),
        "w0_ij": W0[(i * F + j).ravel()],
        "w0_ji": np.concatenate([np.zeros((F, L), W0.dtype), w0_ji]),
        "W1": c(inputs["L0_rec_W1"]),
        "W_top1": c(inputs["W_top1"]),
        "W_top2": c(inputs["W_top2"]),
        "W_top3": c(c(inputs["W_top3"]).reshape(M2 // P, P).T),
        "b_top1": c(c(inputs["b_top1"]).reshape(M1 // P, P).T),
        "b_top2": c(c(inputs["b_top2"]).reshape(M2 // P, P).T),
        "dense_ctx": c(c(inputs["dense_ctx"]).T),
    }
    for f in range(F):
        arrays[f"tbl_{f}"] = c(inputs[f"tbl_{f}"])

    nc = bacc.Bacc("TRN2", target_bir_lowering=False, num_devices=1)
    A = {n: nc.dram_tensor(f"in_{n}", a.shape, mb.dt.from_np(a.dtype), kind="ExternalInput").ap()
         for n, a in arrays.items()}
    y = nc.dram_tensor("out_y", (B, 1), mb.dt.float32, kind="ExternalOutput").ap()
    dlrm_tower(nc, A, y)
    r = run(nc, [{f"in_{n}": a for n, a in arrays.items()}], core_ids=[0])
    return r.results[0]["out_y"]
```

```python
import concourse.bass as bass
from concourse import mybir
from contextlib import ExitStack

F = 39
D = 16
B = 1024
P = 128
NBLK = B // P
DC = 4
NCH = D // DC
CH = DC * P
L = 128
HK = L // 2
PARTS = 3
FP = PARTS * F
NSHIFT = (F + 1) // 2
T0 = -(-NSHIFT // 3)
LAST0 = (NSHIFT - 3 * (T0 - 1)) * F
T1 = -(-F // 2)
PAIR0 = -(-T0 // 2)
PAIR1 = T1 // 2
PAIRS = PAIR0 + PAIR1
ZS = 8
HS = 4
LEAD = 6
AHEAD = 3
TWICE = 2 * F
DVE_K = (1, 3, 5, 7)
POOL_K = (2, 4, 6, 8)
DMA_K = (1, 4, 6, 9)
PE_K = tuple(k for k in range(PAIR1) if k not in DMA_K)
HEAD = 29
M1, M2 = 512, 256
NCTX = 16


def dlrm_tower(nc, A, xt_scratch, y_out):
    fp32, bf16, i32, u32 = mybir.dt.float32, mybir.dt.bfloat16, mybir.dt.int32, mybir.dt.uint32
    fp32r = mybir.dt.float32r
    ALU = mybir.AluOpType
    ACT = mybir.ActivationFunctionType
    AX = mybir.AxisListType

    ctx = ExitStack()
    with ctx:
        def sb(name, shape, dt):
            return ctx.enter_context(nc.sbuf_tensor(name, shape, dt))

        def ps(name, shape, dt):
            return ctx.enter_context(nc.psum_tensor(name, shape, dt))

        def sem(name):
            return ctx.enter_context(nc.semaphore(name))

        ids_all = sb("ids_all", [P, NBLK, F], i32)
        ids_now = sb("ids_now", [P, F], i32)
        emb = sb("emb", [P, F * D], fp32)
        rest = sb("rest", [P, F, D], fp32)
        parts = sb("parts", [P, D, PARTS, F], bf16)
        spread1 = sb("spread1", [FP, T1, L], bf16)
        repeat0 = sb("repeat0", [FP, FP], bf16)
        ident = sb("ident", [P, P], bf16)
        w0 = sb("w0", [FP, T0, L], fp32)
        w1 = sb("w1", [P, T1, L], fp32)
        w1h = sb("w1h", [P, T1, L], fp32r)
        w1l = sb("w1l", [P, T1, L], fp32r)
        xparts = sb("xparts", [FP, NCH, CH], bf16)
        x3 = sb("x3", [FP, NCH, CH], fp32)
        xs = sb("xs", [FP, 2, T0, CH], fp32)
        xw = sb("xw", [P, len(DMA_K), 2, CH], fp32)
        h2 = sb("h2", [P, 2, CH], fp32)
        z = sb("z", [P, ZS, 2, CH], fp32)
        w0_ij, w0_ji = (z[0:FP, n, :, :].rearrange("p a n -> p (a n)")[:, 0:T0 * L].rearrange(
            "p (t l) -> p t l", t=T0) for n in range(2))
        zh = sb("zh", [P, HS, 2, CH], fp32r)
        zl = sb("zl", [P, HS, 2, CH], fp32r)
        sum_d = sb("sum_d", [HK, DC, P], fp32)
        sum_c = sb("sum_c", [L, DC, P], fp32)
        feat_a = sb("feat_a", [HK + NCTX, B], fp32)
        feat_b = sb("feat_b", [L, B], fp32)
        wt1a = sb("wt1a", [HK + NCTX, M1], fp32)
        wt1b = sb("wt1b", [L, M1], fp32)
        wt2 = sb("wt2", [P, M1 // P, M2], fp32)
        wt3 = sb("wt3", [P, M2 // P], fp32)
        b1 = sb("b1", [P, M1 // P], fp32)
        b2 = sb("b2", [P, M2 // P], fp32)
        hid1 = z[:, 0:2, :, :].rearrange("p s t n -> p (s t) n")
        hid2 = z[:, 2, :, :]
        y_row = sb("y_row", [1, B], fp32)

        xb = [ps(f"xb{n}", [P, 2, CH], fp32) for n in range(2)]
        out0 = ps("out0", [P, CH], fp32)
        out1 = ps("out1", [P, CH], fp32)
        t_ps = ps("t_ps", [P, 2 * CH], bf16)
        x3_ps = ps("x3_ps", [P, CH], fp32)

        ids_in = sem("ids_in")
        consts_in = sem("consts_in")
        w0_in = sem("w0_in")
        w0_ready = sem("w0_ready")
        w1_in = sem("w1_in")
        w1_split = sem("w1_split")
        top_in = sem("top_in")
        ids_copied = sem("ids_copied")
        gathered = sem("gathered")
        pool_turns = sem("pool_turns")
        sp_turns = sem("sp_turns")
        xt_out = sem("xt_out")
        xs_in = sem("xs_in")
        xw_in = [sem(f"xw_in{k}") for k in DMA_K]
        split_step = sem("split_step")
        transposed = sem("transposed")
        xparts_ready = sem("xparts_ready")
        x3_made = sem("x3_made")
        x3_ready = sem("x3_ready")
        spread_done = sem("spread_done")
        prod_done = sem("prod_done")
        zh_done = sem("zh_done")
        zl_dve = sem("zl_dve")
        zl_pool = sem("zl_pool")
        pair_used = sem("pair_used")
        h2_ready = sem("h2_ready")
        direct_done = sem("direct_done")
        cur1_done = sem("cur1_done")
        feat_ready = sem("feat_ready")
        mlp1_done = sem("mlp1_done")
        hid1_ready = sem("hid1_ready")
        mlp2_done = sem("mlp2_done")
        hid2_ready = sem("hid2_ready")
        mlp3_done = sem("mlp3_done")
        y_ready = sem("y_ready")
        y_out_done = sem("y_out_done")

        block = ctx.enter_context(nc.Block())

        def step_pairs(c, final):
            l0 = [] if final else [(0, (c + 1) % NCH, k) for k in range(PAIR0)]
            return l0 + [(1, c, k) for k in range(PAIR1)]

        def lead(final):
            return PAIR0 + 1 if final else LEAD

        def following(c, last):
            if last and c == NCH - 1:
                return []
            final = last and c + 1 == NCH - 1
            return step_pairs((c + 1) % NCH, final)[:lead(final)]

        def pair_number(blk, c, pos):
            return blk * (NCH * PAIRS) + (PAIR0 + c * PAIRS + pos)

        def z_slot(c, pos):
            return (PAIR0 + c * PAIRS + pos) % ZS

        def split_pairs(first):
            return sorted(DVE_K if first else DVE_K + POOL_K)

        def split_number(blk, c, k, first):
            nth = split_pairs(first).index(k)
            if first:
                return c * len(DVE_K) + nth
            each = len(split_pairs(False))
            return blk * (NCH * each) + (c * each + nth - NCH * len(POOL_K))

        def split_slot(c, k, first):
            return split_number(0 if first else 1, c, k, first) % HS

        def split_slot_before(c, k, first):
            pairs = split_pairs(first)
            nth = pairs.index(k) - HS
            if nth < 0 and c == 0 and not first:
                assert split_pairs(True)[nth] <= pairs[nth]
            return nth < 0, pairs[nth]

        def tiles_of(layer, k):
            count = T0 if layer == 0 else T1
            return [t for t in (2 * k, 2 * k + 1) if t < count]

        @block.sync
        def _(sp):
            sp.dma_start(ids_all[:], A["ids"].rearrange("(n p) f -> p n f", p=P)).then_inc(ids_in, 16)
            sp.dma_start(ident[:], A["ident"]).then_inc(consts_in, 16)
            sp.dma_start(repeat0[:], A["repeat0"]).then_inc(consts_in, 16)
            sp.dma_start(spread1[:], A["spread1"].rearrange("p (t m) -> p t m", t=T1)).then_inc(consts_in, 16)
            full = (T0 - 1) * FP
            for src, dst in ((A["w0_ij"], w0_ij), (A["w0_ji"], w0_ji)):
                sp.dma_start(dst[:, 0:T0 - 1, :],
                             src[0:full, :].rearrange("(t p) l -> p t l", p=FP)).then_inc(w0_in, 16)
                sp.dma_start(dst[0:LAST0, T0 - 1, :], src[full:full + LAST0, :]).then_inc(w0_in, 16)
            full = (T1 - 1) * P
            sp.dma_start(w1[:, 0:T1 - 1, :],
                         A["W1"][0:full, :].rearrange("(t p) l -> p t l", p=P)).then_inc(w1_in, 16)
            sp.dma_start(w1[0:HK, T1 - 1, :], A["W1"][full:full + HK, :]).then_inc(w1_in, 16)
            sp.dma_start(wt1a[0:HK, :], A["W_top1"][0:HK, :]).then_inc(top_in, 16)
            sp.dma_start(wt1a[HK:HK + NCTX, :], A["W_top1"][HK + L:HK + L + NCTX, :]).then_inc(top_in, 16)
            sp.dma_start(wt1b[:], A["W_top1"][HK:HK + L, :]).then_inc(top_in, 16)
            sp.dma_start(wt2[:], A["W_top2"].rearrange("(k p) n -> p k n", p=P)).then_inc(top_in, 16)
            sp.dma_start(wt3[:], A["W_top3"]).then_inc(top_in, 16)
            sp.dma_start(b1[:], A["b_top1"]).then_inc(top_in, 16)
            sp.dma_start(b2[:], A["b_top2"]).then_inc(top_in, 16)
            sp.dma_start(feat_a[HK:HK + NCTX, :], A["dense_ctx"]).then_inc(top_in, 16)

            def sp_wait(semaphore, value):
                sp.wait_ge(semaphore, value)
                sp.sem_inc(sp_turns, 1)

            def shift_chunk(blk, c, early):
                m = blk * NCH + c
                if not (early and c == 0):
                    sp_wait(xs_in, m * 48)
                sp_wait(x3_ready, m + 1)
                sp.dma_start(xt_scratch[c, :, :], x3[0:TWICE, c, :]).then_inc(xt_out, 16)
                if early and c == 2:
                    sp_wait(prod_done, PAIR0)
                elif not early or c > 2:
                    sp_wait(prod_done, pair_number(blk, c, 0) - 3 * PAIRS + PAIR0)
                sp_wait(xt_out, m * 16 + 16)
                for n in range(3):
                    tiles = T0 if n < NSHIFT - 3 * (T0 - 1) else T0 - 1
                    rows = bass.AP(tensor=xt_scratch.tensor,
                                   offset=xt_scratch.offset + (c * TWICE + n) * CH,
                                   ap=[[CH, F], [3 * CH, tiles], [1, CH]])
                    sp.dma_start(xs[n * F:(n + 1) * F, c % 2, 0:tiles, :], rows).then_inc(xs_in, 16)

            def spread_pair(j, c):
                for half in range(2):
                    rows = bass.AP(tensor=xt_scratch.tensor,
                                   offset=xt_scratch.offset + (c * TWICE + 4 * DMA_K[j] + half) * CH,
                                   ap=[[0, HK], [2 * CH, 2], [1, CH]])
                    sp.dma_start(xw[half * HK:(half + 1) * HK, j, :, :], rows).then_inc(xw_in[j], 16)

            def step(blk, c, first, last):
                for j, k in enumerate(DMA_K):
                    if not (last and c == NCH - 1):
                        sp_wait(prod_done, pair_number(blk, c, PAIR0 + k) + 1)
                        spread_pair(j, (c + 1) % NCH)
                if not last or c == 0:
                    shift_chunk(blk + (c + AHEAD) // NCH, (c + AHEAD) % NCH, first and c == 0)

            shift_chunk(0, 0, True)
            for j in range(len(DMA_K)):
                spread_pair(j, 0)
            shift_chunk(0, 1, True)
            shift_chunk(0, 2, True)
            for c in range(NCH):
                step(0, c, True, False)
            with sp.Fori(1, NBLK - 1) as blk:
                for c in range(NCH):
                    step(blk, c, False, False)
            for c in range(NCH):
                step(NBLK - 1, c, False, True)
            sp.wait_ge(y_ready, 2)
            sp.dma_start(y_out.rearrange("b o -> o b"), y_row[:]).then_inc(y_out_done, 16)
            sp.wait_ge(y_out_done, 16)

        def part(n):
            return parts[:, :, n, :].rearrange("p d f -> p f d")

        @block.gpsimd
        def _(pool):
            def stand_alone():
                pool.sem_inc(pool_turns, 1)

            def next_ids(blk):
                pool.wait_ge(gathered, blk * (16 * F))
                pool.wait_ge(split_step, blk * 4 - 2)
                stand_alone()
                nc.gpsimd.tensor_copy(ids_now[:], ids_all[:, bass.ds(blk, 1), :].rearrange(
                    "p o f -> p (o f)")).then_inc(ids_copied, 1)
                pool.wait_ge(ids_copied, blk + 1)
                stand_alone()

            def gather(fields):
                for f in fields:
                    nc.gpsimd.indirect_dma_start(
                        out=emb[:, f * D:(f + 1) * D], out_offset=None, in_=A[f"tbl_{f}"],
                        in_offset=bass.IndirectOffsetOnAxis(ap=ids_now[:, f:f + 1].bitcast(u32), axis=0),
                    ).then_inc(gathered, 16)

            def low_half(blk, c, k):
                final = blk is NBLK - 1 and c == NCH - 1
                pool.wait_ge(zh_done, split_number(blk, c, k, False) + 1)
                zs, hs = z_slot(c, k if final else PAIR0 + k), split_slot(c, k, False)
                nc.gpsimd.tensor_tensor(zl[:, hs, :, :], z[:, zs, :, :],
                                        zh[:, hs, :, :].bitcast(fp32), ALU.subtract).then_inc(zl_pool, 1)

            def run_block(blk, gather_tail, gather_next):
                fields = list(range(HEAD, F)) if gather_tail else []
                for c in range(NCH):
                    for k in POOL_K:
                        low_half(blk, c, k)
                        if c == 1 and k == 6 and gather_next:
                            next_ids(blk + 2)
                            fields = list(range(HEAD))
                        some = 1 if k != POOL_K[-1] else 8 if c == 3 else 7
                        gather(fields[:some])
                        fields = fields[some:]
                assert not fields

            pool.wait_ge(ids_in, 16)
            nc.gpsimd.tensor_copy(ids_now[:], ids_all[:, 0, :]).then_inc(ids_copied, 1)
            pool.wait_ge(ids_copied, 1)
            gather(range(F))
            next_ids(1)
            gather(range(F))
            next_ids(2)
            gather(range(HEAD))
            with pool.Fori(1, NBLK - 2) as blk:
                run_block(blk, True, True)
            run_block(NBLK - 2, True, False)
            run_block(NBLK - 1, False, False)

        @block.tensor
        def _(pe):
            def transpose_chunk(chunk_no, block_no, c):
                pe.wait_ge(split_step, block_no * 4 + 4)
                pe.wait_ge(xparts_ready, chunk_no)
                for q in range(DC):
                    last = nc.tensor.transpose(
                        t_ps[0:FP, q * P:(q + 1) * P],
                        parts[:, c * DC + q, :, :].rearrange("p a f -> p (a f)"), ident[:])
                last.then_inc(transposed, 1)

            def make_x3(chunk_no, c):
                pe.wait_ge(xparts_ready, chunk_no + 1)
                pe.wait_ge(x3_ready, chunk_no)
                nc.tensor.matmul(x3_ps[0:FP, :], repeat0[:], xparts[:, c, :],
                                 start=True, stop=True).then_inc(x3_made, 1)

            def spread(c, k):
                slot = PE_K.index(k) % 2
                for n, t in enumerate(tiles_of(1, k)):
                    last = nc.tensor.matmul(xb[slot][:, n, :], spread1[:, t, :], xparts[:, c, :],
                                            start=True, stop=True)
                last.then_inc(spread_done, 1)

            def contract_0(k, zs):
                for n, t in enumerate(tiles_of(0, k)):
                    rows = FP if t < T0 - 1 else LAST0
                    last = nc.tensor.matmul(out0[:], w0[0:rows, t, :], z[0:rows, zs, n, :],
                                            start=(t == 0), stop=(t == T0 - 1))
                last.then_inc(pair_used, 1)

            def contract_1(k, zs, hs):
                for n, t in enumerate(tiles_of(1, k)):
                    rows = P if t < T1 - 1 else HK
                    start, stop = t == 0, t == T1 - 1
                    if hs is None:
                        last = nc.tensor.matmul(out1[:], w1[0:rows, t, :], z[0:rows, zs, n, :],
                                                start=start, stop=stop)
                    else:
                        for w, x in ((w1h, zh), (w1h, zl), (w1l, zh)):
                            last = nc.tensor.matmul(
                                out1[:], w[0:rows, t, :], x[0:rows, hs, n, :],
                                start=start and w is w1h and x is zh, stop=stop and w is w1l)
                last.then_inc(pair_used, 1)

            def step(blk, c, first, last):
                final = last and c == NCH - 1
                l0_pairs = 0 if final else PAIR0
                number = lambda pos: pair_number(blk, c, pos)

                def spread_ahead(k):
                    before = PE_K[PE_K.index(k) - 2]
                    pe.wait_ge(prod_done, number(l0_pairs + before) + 1)
                    spread(c, k)

                if final:
                    for k in PE_K[2:]:
                        if k < PAIR0:
                            spread_ahead(k)
                for pos, (layer, slot, k) in enumerate(step_pairs(c, final)):
                    ahead = pos + (PAIR0 if final else 0)
                    if ahead in PE_K[2:]:
                        spread_ahead(ahead)
                    if pos >= PAIRS - 2:
                        nth = pos - (PAIRS - 2)
                        pe.wait_ge(prod_done, number(PAIR0 + PE_K[nth - 2]) + 1)
                        spread((c + 1) % NCH, PE_K[nth])
                    if layer == 0:
                        if k == 0:
                            pe.wait_ge(h2_ready, (blk * NCH + c + 1) * 2)
                            pe.wait_ge(direct_done, blk * NCH + c + 1)
                        pe.wait_ge(prod_done, number(pos) + 1)
                        contract_0(k, z_slot(c, pos))
                    else:
                        if k == 0:
                            pe.wait_ge(cur1_done, blk * NCH + c + 1)
                        split = k in split_pairs(first)
                        if not split:
                            pe.wait_ge(prod_done, number(pos) + 1)
                        elif k in DVE_K:
                            pe.wait_ge(zl_dve, (blk * NCH + c) * len(DVE_K) + (DVE_K.index(k) + 1))
                        else:
                            pe.wait_ge(zl_pool, (blk * NCH + c) * len(POOL_K)
                                       + (POOL_K.index(k) + 1 - NCH * len(POOL_K)))
                        contract_1(k, z_slot(c, pos), split_slot(c, k, first) if split else None)
                    if not last or c == 0:
                        chunk, to = blk * NCH + (c + AHEAD), (c + AHEAD) % NCH
                        if pos == PAIRS - 3:
                            transpose_chunk(chunk, blk + (c + AHEAD) // NCH, to)
                        if pos == PAIRS - 1:
                            make_x3(chunk, to)

            pe.sem_inc(transposed, 1)
            pe.wait_ge(consts_in, 48)
            for c in range(AHEAD):
                transpose_chunk(c, 0, c)
                make_x3(c, c)
            for k in PE_K[:2]:
                spread(0, k)
            pe.wait_ge(w0_ready, 2)
            for k in range(PAIR0):
                pe.wait_ge(prod_done, k + 1)
                contract_0(k, k)
            pe.wait_ge(w1_in, 32)
            pe.wait_ge(w1_split, 2)
            for c in range(NCH):
                step(0, c, True, False)
            with pe.Fori(1, NBLK - 1) as blk:
                for c in range(NCH):
                    step(blk, c, False, False)
            for c in range(NCH):
                step(NBLK - 1, c, False, True)

            pe.wait_ge(top_in, 128)
            pe.wait_ge(feat_ready, 2 * NBLK)
            n1, n2 = M1 // P, M2 // P
            for half in range(B // CH):
                cols = slice(half * CH, (half + 1) * CH)
                for m in range(n1):
                    if half:
                        pe.wait_ge(hid1_ready, m + 1)
                    dst = xb[m // 2][:, m % 2, :]
                    nc.tensor.matmul(dst, wt1a[:, m * P:(m + 1) * P], feat_a[:, cols], start=True, stop=False)
                    nc.tensor.matmul(dst, wt1b[:, m * P:(m + 1) * P], feat_b[:, cols],
                                     start=False, stop=True).then_inc(mlp1_done, 1)
                pe.wait_ge(hid1_ready, n1 * (half + 1))
                for m in range(n2):
                    if half:
                        pe.wait_ge(hid2_ready, m + 1)
                    dst = (out0, out1)[m]
                    for k in range(n1):
                        last = nc.tensor.matmul(dst[:], wt2[:, k, m * P:(m + 1) * P], hid1[:, k, :],
                                                start=(k == 0), stop=(k == n1 - 1))
                    last.then_inc(mlp2_done, 1)
                pe.wait_ge(hid2_ready, n2 * (half + 1))
                if half:
                    pe.wait_ge(y_ready, half)
                for k in range(n2):
                    last = nc.tensor.matmul(x3_ps[0:1, :], wt3[:, k:k + 1], hid2[:, k, :],
                                            start=(k == 0), stop=(k == n2 - 1))
                last.then_inc(mlp3_done, 1)

        @block.scalar
        def _(act):
            def copy_xparts(chunk_no, c):
                act.wait_ge(transposed, chunk_no + 2)
                nc.scalar.copy(xparts[:, c, :], t_ps[0:FP, 0:CH]).then_inc(xparts_ready, 1)

            def copy_x3(chunk_no, c):
                act.wait_ge(x3_made, chunk_no + 1)
                nc.scalar.copy(x3[:, c, :], x3_ps[0:FP, :]).then_inc(x3_ready, 1)

            def relu_next(pairs_used, slot):
                act.wait_ge(pair_used, pairs_used)
                for half in range(2):
                    nc.scalar.activation(h2[half * HK:(half + 1) * HK, slot, :], out0[HK:L, :],
                                         ACT.Relu).then_inc(h2_ready, 1)

            def split_part(blk, n):
                if n == 0:
                    act.wait_ge(gathered, (blk + 1) * (16 * F))
                    act.wait_ge(transposed, blk * NCH + 1)
                    nc.scalar.copy(part(0), emb[:].rearrange("p (f d) -> p f d", f=F)).then_inc(split_step, 1)
                else:
                    act.wait_ge(split_step, blk * 4 + 2)
                    nc.scalar.copy(part(1), rest[:]).then_inc(split_step, 1)

            def high_half(blk, c, k, first, final):
                pos = k if final else PAIR0 + k
                act.wait_ge(prod_done, pair_number(blk, c, pos) + 1)
                earlier, before = split_slot_before(c, k, first)
                if not (first and c == 0 and earlier):
                    back = k - before + (PAIR0 + PAIR1 if earlier else 0) - (PAIR0 if earlier and final else 0)
                    act.wait_ge(pair_used, pair_number(blk, c, pos - back) + 1)
                hs = split_slot(c, k, first)
                nc.scalar.copy(zh[:, hs, :, :], z[:, z_slot(c, pos), :, :]).then_inc(zh_done, 1)

            def step(blk, c, first, last):
                final = last and c == NCH - 1
                for k in range(PAIR1):
                    if k in split_pairs(first):
                        high_half(blk, c, k, first, final)
                    if c == 1 and not last and k in (2, 5):
                        split_part(blk + 1, 0 if k == 2 else 1)
                    if k == 4 and not final:
                        relu_next(pair_number(blk, c, PAIR0), (c + 1) % 2)
                if not last or c == 0:
                    chunk, to = blk * NCH + (c + AHEAD), (c + AHEAD) % NCH
                    copy_xparts(chunk, to)
                    copy_x3(chunk, to)

            act.wait_ge(w1_in, 32)
            nc.scalar.copy(w1h[:, 0:T1 - 1, :], w1[:, 0:T1 - 1, :])
            nc.scalar.copy(w1h[0:HK, T1 - 1, :], w1[0:HK, T1 - 1, :]).then_inc(w1_split, 1)
            split_part(0, 0)
            split_part(0, 1)
            for c in range(AHEAD):
                copy_xparts(c, c)
                copy_x3(c, c)
            relu_next(PAIR0, 0)
            for c in range(NCH):
                step(0, c, True, False)
            with act.Fori(1, NBLK - 1) as blk:
                for c in range(NCH):
                    step(blk, c, False, False)
            for c in range(NCH):
                step(NBLK - 1, c, False, True)

            n1, n2 = M1 // P, M2 // P
            act.wait_ge(top_in, 128)
            for half in range(B // CH):
                for m in range(n1):
                    act.wait_ge(mlp1_done, half * n1 + m + 1)
                    if half:
                        act.wait_ge(mlp2_done, n2)
                    nc.scalar.activation(hid1[:, m, :], xb[m // 2][:, m % 2, :], ACT.Relu,
                                         bias=b1[:, m:m + 1]).then_inc(hid1_ready, 1)
                for m in range(n2):
                    act.wait_ge(mlp2_done, half * n2 + m + 1)
                    if half:
                        act.wait_ge(mlp3_done, 1)
                    nc.scalar.activation(hid2[:, m, :], (out0, out1)[m][:], ACT.Relu,
                                         bias=b2[:, m:m + 1]).then_inc(hid2_ready, 1)
                act.wait_ge(mlp3_done, half + 1)
                nc.scalar.copy(y_row[0:1, half * CH:(half + 1) * CH], x3_ps[0:1, :]).then_inc(y_ready, 1)

        @block.vector
        def _(dve):
            dve.sem_inc(cur1_done, 1)
            dve.wait_ge(w0_in, 64)
            for half in range(2):
                to, frm = slice(half * HK, (half + 1) * HK), slice((1 - half) * HK, (2 - half) * HK)
                nc.vector.tensor_tensor(w0[:, 0:T0 - 1, to], w0_ij[:, 0:T0 - 1, frm],
                                        w0_ji[:, 0:T0 - 1, frm], ALU.add)
                last = nc.vector.tensor_tensor(w0[0:LAST0, T0 - 1, to], w0_ij[0:LAST0, T0 - 1, frm],
                                               w0_ji[0:LAST0, T0 - 1, frm], ALU.add)
                last.then_inc(w0_ready, 1)

            def product(pair, number, zslot, l0_chunk, l1_chunk, free):
                layer, c, k = pair
                n = len(tiles_of(layer, k))
                if layer == 0:
                    rows = FP if k < PAIR0 - 1 else LAST0
                    own, fixed = xs[0:rows, c % 2, 2 * k:2 * k + n, :], x3[0:rows, c, :]
                    if k == 0:
                        dve.wait_ge(x3_ready, l0_chunk + 1)
                        dve.wait_ge(xs_in, l0_chunk * 48 + 48)
                else:
                    rows, fixed = P, h2[:, c % 2, :]
                    if k == 0:
                        dve.wait_ge(h2_ready, l1_chunk * 2 + 2)
                    if k in DMA_K:
                        own = xw[:, DMA_K.index(k), :, :]
                        dve.wait_ge(xw_in[DMA_K.index(k)], l1_chunk * 32 + 32)
                    else:
                        own = xb[PE_K.index(k) % 2][:]
                        dve.wait_ge(spread_done, l1_chunk * len(PE_K) + (PE_K.index(k) + 1))
                if free:
                    dve.wait_ge(pair_used, number - (ZS - 1))
                nc.vector.tensor_tensor(z[0:rows, zslot, 0:n, :], own,
                                        fixed.unsqueeze(1).to_broadcast([rows, n, CH]),
                                        ALU.mult).then_inc(prod_done, 1)

            def low_half(blk, c, k, first, final):
                dve.wait_ge(zh_done, split_number(blk, c, k, first) + 1)
                zs, hs = z_slot(c, k if final else PAIR0 + k), split_slot(c, k, first)
                nc.vector.tensor_tensor(zl[:, hs, :, :], z[:, zs, :, :],
                                        zh[:, hs, :, :].bitcast(fp32), ALU.subtract).then_inc(zl_dve, 1)

            def split_rest(blk, n):
                if n == 0:
                    dve.wait_ge(split_step, blk * 4 + 1)
                    nc.vector.tensor_tensor(rest[:], emb[:].rearrange("p (f d) -> p f d", f=F),
                                            part(0), ALU.subtract).then_inc(split_step, 1)
                else:
                    dve.wait_ge(split_step, blk * 4 + 3)
                    nc.vector.tensor_tensor(part(2), rest[:], part(1),
                                            ALU.subtract).then_inc(split_step, 1)

            def add_direct(blk, chunk_no, c, pairs_used):
                dve.wait_ge(pair_used, pairs_used)
                flat = sum_d[:].rearrange("l q b -> l (q b)")
                if c == 0:
                    nc.vector.tensor_scalar(flat, out0[0:HK, :], 0.0, None, ALU.max).then_inc(direct_done, 1)
                else:
                    dve.wait_ge(direct_done, chunk_no)
                    nc.vector.scalar_tensor_tensor(flat, out0[0:HK, :], 0.0, flat,
                                                   ALU.max, ALU.add).then_inc(direct_done, 1)
                if c == NCH - 1:
                    dve.wait_ge(direct_done, chunk_no + 1)
                    nc.vector.tensor_reduce(feat_a[0:HK, bass.ds(blk * P, P)],
                                            sum_d[:].rearrange("l q b -> l b q"),
                                            AX.X, ALU.add).then_inc(feat_ready, 1)

            def add_cur1(blk, chunk_no, c, pairs_used):
                dve.wait_ge(pair_used, pairs_used)
                flat = sum_c[:].rearrange("l q b -> l (q b)")
                if c == 0:
                    nc.vector.tensor_scalar(flat, out1[:], 0.0, None, ALU.max).then_inc(cur1_done, 1)
                else:
                    dve.wait_ge(cur1_done, chunk_no + 1)
                    nc.vector.scalar_tensor_tensor(flat, out1[:], 0.0, flat,
                                                   ALU.max, ALU.add).then_inc(cur1_done, 1)
                if c == NCH - 1:
                    dve.wait_ge(cur1_done, chunk_no + 2)
                    nc.vector.tensor_reduce(feat_b[:, bass.ds(blk * P, P)],
                                            sum_c[:].rearrange("l q b -> l b q"),
                                            AX.X, ALU.add).then_inc(feat_ready, 1)

            def step(blk, c, first, last):
                final = last and c == NCH - 1
                pairs = step_pairs(c, final)
                ahead = pairs + following(c, last)
                chunk = blk * NCH + c
                for pos in range(lead(final), len(ahead) + 1):
                    if pos < len(ahead):
                        nxt = pos >= len(pairs)
                        product(ahead[pos], pair_number(blk, c, pos), z_slot(c, pos),
                                chunk + (2 if nxt else 1), chunk + (1 if nxt else 0), True)
                    layer, slot, k = ahead[pos - 1]
                    if layer == 1 and k in DVE_K and (pos < len(ahead) or final):
                        low_half(blk, slot, k, first, final or slot != c)
                    if pos == PAIR0 + 5 and not final:
                        add_direct(blk if c < NCH - 1 else blk + 1, chunk + 1, (c + 1) % NCH,
                                   pair_number(blk, c, PAIR0))
                    if c == 1 and not last and pos in (PAIR0 + 4, PAIR0 + 7):
                        split_rest(blk + 1, 0 if pos == PAIR0 + 4 else 1)
                add_cur1(blk, chunk, c, pair_number(blk, c, len(pairs)))

            dve.wait_ge(w1_split, 1)
            nc.vector.tensor_tensor(w1l[:, 0:T1 - 1, :], w1[:, 0:T1 - 1, :],
                                    w1h[:, 0:T1 - 1, :].bitcast(fp32), ALU.subtract)
            nc.vector.tensor_tensor(w1l[0:HK, T1 - 1, :], w1[0:HK, T1 - 1, :],
                                    w1h[0:HK, T1 - 1, :].bitcast(fp32), ALU.subtract).then_inc(w1_split, 1)
            split_rest(0, 0)
            split_rest(0, 1)
            opening = [(0, 0, k) for k in range(PAIR0)] + step_pairs(0, False)[:LEAD]
            for n, pair in enumerate(opening):
                if n == PAIR0:
                    add_direct(0, 0, 0, PAIR0)
                product(pair, n, n % ZS, 0 if n < PAIR0 else 1, 0, n >= ZS)
            for c in range(NCH):
                step(0, c, True, False)
            with dve.Fori(1, NBLK - 1) as blk:
                for c in range(NCH):
                    step(blk, c, False, False)
            for c in range(NCH):
                step(NBLK - 1, c, False, True)


def kernel(**inputs):
    import numpy as np
    import ml_dtypes
    import concourse.bacc as bacc
    from concourse import mybir as mb
    from concourse.bass_utils import run_bass_kernel_spmd as run

    def c(a):
        return np.ascontiguousarray(np.asarray(a))

    field = np.arange(FP) % F
    one = ml_dtypes.bfloat16
    spread1 = np.stack([field[:, None] == (2 * t + np.arange(L) // HK).clip(max=F - 1)[None, :]
                        for t in range(T1)], 1)
    s, i = np.meshgrid(np.arange(NSHIFT), np.arange(F), indexing="ij")
    j = (i + s) % F
    W0 = c(inputs["L0_rec_W0"])
    w0_ji = W0[(j * F + i).ravel()[F:]]

    arrays = {
        "ids": c(inputs["ids"]),
        "ident": np.eye(P, dtype=one),
        "repeat0": (field[:, None] == field[None, :]).astype(one),
        "spread1": spread1.reshape(FP, T1 * L).astype(one),
        "w0_ij": W0[(i * F + j).ravel()],
        "w0_ji": np.concatenate([np.zeros((F, L), W0.dtype), w0_ji]),
        "W1": c(inputs["L0_rec_W1"]),
        "W_top1": c(inputs["W_top1"]),
        "W_top2": c(inputs["W_top2"]),
        "W_top3": c(c(inputs["W_top3"]).reshape(M2 // P, P).T),
        "b_top1": c(c(inputs["b_top1"]).reshape(M1 // P, P).T),
        "b_top2": c(c(inputs["b_top2"]).reshape(M2 // P, P).T),
        "dense_ctx": c(c(inputs["dense_ctx"]).T),
    }
    for f in range(F):
        arrays[f"tbl_{f}"] = c(inputs[f"tbl_{f}"])

    nc = bacc.Bacc("TRN2", target_bir_lowering=False, num_devices=1)
    A = {n: nc.dram_tensor(f"in_{n}", a.shape, mb.dt.from_np(a.dtype), kind="ExternalInput").ap()
         for n, a in arrays.items()}
    y = nc.dram_tensor("out_y", (B, 1), mb.dt.float32, kind="ExternalOutput").ap()
    xt_scratch = nc.dram_tensor("xt_scratch", (NCH, TWICE, CH), mb.dt.float32).ap()
    dlrm_tower(nc, A, xt_scratch, y)
    r = run(nc, [{f"in_{n}": a for n, a in arrays.items()}], core_ids=[0])
    return r.results[0]["out_y"]
```

```python
import concourse.bass as bass
from concourse import mybir
from contextlib import ExitStack

F = 39
D = 16
B = 1024
P = 128
NBLK = B // P
DC = 4
NCH = D // DC
CH = DC * P
L = 128
HK = L // 2
PARTS = 3
FP = PARTS * F
NSHIFT = (F + 1) // 2
T0 = -(-NSHIFT // 3)
LAST0 = (NSHIFT - 3 * (T0 - 1)) * F
T1 = -(-F // 2)
PAIR0 = -(-T0 // 2)
PAIR1 = T1 // 2
PAIRS = PAIR0 + PAIR1
ZS = 8
HS = 4
LEAD = 7
AHEAD = 3
TWICE = 2 * F
DVE_K = (2, 4, 6, 8)
POOL_K = (1, 3, 5, 7, 9)
DMA_K = (1, 3, 4, 5, 7, 9)
PE_K = tuple(k for k in range(PAIR1) if k not in DMA_K)
XB = 2
NLOOK = 15
LK = 125
EARLY = 2
HEAD = 28
M1, M2 = 512, 256
NCTX = 16


def dlrm_tower(nc, A, xt_scratch, y_out):
    fp32, bf16, i32, u32 = mybir.dt.float32, mybir.dt.bfloat16, mybir.dt.int32, mybir.dt.uint32
    fp32r = mybir.dt.float32r
    ALU = mybir.AluOpType
    ACT = mybir.ActivationFunctionType
    AX = mybir.AxisListType

    ctx = ExitStack()
    with ctx:
        def sb(name, shape, dt):
            return ctx.enter_context(nc.sbuf_tensor(name, shape, dt))

        def ps(name, shape, dt):
            return ctx.enter_context(nc.psum_tensor(name, shape, dt))

        def sem(name):
            return ctx.enter_context(nc.semaphore(name))

        table_rows = [A[f"tbl_{f}"].shape[0] for f in range(F)]
        lookup = sorted((f for f in range(F) if table_rows[f] in (8 * LK, 10 * LK)),
                        key=lambda f: table_rows[f])[:NLOOK]
        assert len(lookup) == NLOOK
        tiles_in = {f: table_rows[f] // LK for f in lookup}
        groups = []
        for f in lookup:
            if (not groups or tiles_in[f] != tiles_in[groups[-1][0]]
                    or (len(groups[-1]) + 1) * tiles_in[f] > 32):
                groups.append([])
            groups[-1].append(f)
        NG = len(groups)

        ids_all = sb("ids_all", [P, NBLK, F], i32)
        ids_now = sb("ids_now", [P, F], i32)
        emb = sb("emb", [P, F * D], fp32)
        rest = sb("rest", [P, F, D], fp32)
        parts = sb("parts", [P, D, PARTS, F], bf16)
        spread1 = sb("spread1", [FP, T1, L], bf16)
        repeat0 = sb("repeat0", [FP, FP], bf16)
        ident = sb("ident", [P, P], bf16)
        w0 = sb("w0", [FP, T0, L], fp32)
        w1 = sb("w1", [P, T1, L], fp32)
        w1h = sb("w1h", [P, T1 - 1, L], fp32r)
        w1l = sb("w1l", [P, T1 - 1, L], fp32r)
        xparts = sb("xparts", [FP, NCH, CH], bf16)
        x3 = sb("x3", [FP, 2, CH], fp32)
        xs = sb("xs", [P, 2, T0, CH], fp32)
        xw = sb("xw", [P, len(DMA_K), 2, CH], fp32)
        h2 = sb("h2", [P, 2, CH], fp32)
        z = sb("z", [P, ZS, 2, CH], fp32)
        zh = sb("zh", [P, HS, 2, CH], fp32r)
        zl = sb("zl", [P, HS, 2, CH], fp32r)
        shift0 = sb("shift0", [FP, T0, FP], bf16)
        xw_flat = xw[:].rearrange("p s a n -> p (s a n)")
        start_of = {}
        for f in lookup:
            start_of[f] = sum(tiles_in[e] * D for e in start_of)
        width = sum(tiles_in[f] * D for f in lookup)
        table_rest = xw_flat[0:LK, width:2 * width]
        xs_flat = xs[:].rearrange("p s t n -> p (s t n)")
        look_ids = xs_flat[0:LK, 0:NLOOK * P].bitcast(i32)
        table_parts = xs_flat[:, NLOOK * P:].bitcast(bf16)[0:LK, 0:PARTS * width]
        one_hot = z[:, 4:8, :, :].rearrange("p (r s) a n -> p r (s a n)", r=2).bitcast(bf16)
        row_no = sb("row_no", [LK, 18], fp32)

        def group_cols(group):
            return slice(start_of[group[0]], start_of[group[-1]] + tiles_in[group[-1]] * D)

        def table_part(n, cols):
            return table_parts[:, n * width + cols.start:n * width + cols.stop]

        def one_hot_tile(g, t):
            n = len(groups[g]) * P
            return one_hot[0:LK, g % 2, t * n:(t + 1) * n]
        wt = z[:, 2:4, :, :].rearrange("p s a n -> p (s a n)")
        wt1a, wt1b = wt[0:HK + NCTX, 0:M1], wt[:, M1:2 * M1]
        wt2 = wt[:, 2 * M1:].rearrange("p (k n) -> p k n", k=M1 // P)
        w0_ij, w0_ji = (z[0:FP, n, :, :].rearrange("p a n -> p (a n)")[:, 0:T0 * L].rearrange(
            "p (t l) -> p t l", t=T0) for n in range(2))
        sum_d = sb("sum_d", [HK, DC, P], fp32)
        sum_c = sb("sum_c", [L, DC, P], fp32)
        feat_a = sb("feat_a", [HK + NCTX, B], fp32)
        feat_b = sb("feat_b", [L, B], fp32)
        wth = sb("wth", [P, 2 * M1 + M1 // P * M2], fp32r)
        wtl = sb("wtl", [P, 2 * M1 + M1 // P * M2], fp32r)
        wt3 = sb("wt3", [P, M2 // P], fp32)
        b1 = sb("b1", [P, M1 // P], fp32)
        b2 = sb("b2", [P, M2 // P], fp32)
        hid1 = [z[:, 2 * n:2 * n + 2, :, :].rearrange("p s t n -> p (s t) n") for n in range(2)]
        hid2 = [z[:, 4 + n, :, :] for n in range(2)]
        FEAT_SLOT = (0, 3)
        HID1_SLOT = ((1, 2), (0, 1))
        y_row = w1[0:1, 0:B // L, :].rearrange("p t l -> p (t l)")

        xb = [ps(f"xb{n}", [P, 2, CH], fp32) for n in range(XB)]
        out0 = ps("out0", [P, CH], fp32)
        out1 = ps("out1", [P, CH], fp32)
        x3_ps = ps("x3_ps", [P, CH], fp32)
        t_ps = ps("t_ps", [P, 2 * CH], bf16)
        mlp3_ps = (x3_ps, t_ps[:].bitcast(fp32))

        look_bank = [xb[0][:, 0, :], xb[0][:, 1, :], xb[1][:, 0, :], xb[1][:, 1, :], out0[:], out1[:]][0:NG]

        ids_in = sem("ids_in")
        look_ids_in = sem("look_ids_in")
        table_in = [sem(f"table_in{g}") for g in range(NG)]
        table_high = sem("table_high")
        table_low = sem("table_low")
        one_hot_ready = sem("one_hot_ready")
        look_done = sem("look_done")
        looked_up = sem("looked_up")
        consts_in = sem("consts_in")
        w0_in = sem("w0_in")
        w0_ready = sem("w0_ready")
        w1_in = sem("w1_in")
        w1_split = sem("w1_split")
        wt_in = sem("wt_in")
        top_in = sem("top_in")
        ids_copied = sem("ids_copied")
        gathered = sem("gathered")
        pool_turns = sem("pool_turns")
        sp_turns = sem("sp_turns")
        xt_out = sem("xt_out")
        xs_in = sem("xs_in")
        xw_in = [sem(f"xw_in{k}") for k in DMA_K]
        split_step = sem("split_step")
        transposed = sem("transposed")
        xparts_ready = sem("xparts_ready")
        x3_made = sem("x3_made")
        x3_ready = sem("x3_ready")
        shifted = sem("shifted")
        spread_done = sem("spread_done")
        prod_done = sem("prod_done")
        zh_done = sem("zh_done")
        zl_dve = sem("zl_dve")
        zl_pool = sem("zl_pool")
        pair_used = sem("pair_used")
        h2_ready = sem("h2_ready")
        direct_done = sem("direct_done")
        cur1_done = sem("cur1_done")
        feat_ready = sem("feat_ready")
        wt_split = sem("wt_split")
        feat_high = sem("feat_high")
        feat_low = sem("feat_low")
        mlp1_done = sem("mlp1_done")
        hid1_ready = sem("hid1_ready")
        hid1_low = sem("hid1_low")
        mlp2_done = sem("mlp2_done")
        hid2_ready = sem("hid2_ready")
        mlp3_done = sem("mlp3_done")
        y_ready = sem("y_ready")
        y_out_done = sem("y_out_done")

        block = ctx.enter_context(nc.Block())

        def step_pairs(c, final):
            l0 = [] if final else [(0, (c + 1) % NCH, k) for k in range(PAIR0)]
            return l0 + [(1, c, k) for k in range(PAIR1)]

        def lead(final):
            return PAIR0 + 1 if final else LEAD

        def following(c, last):
            if last and c == NCH - 1:
                return []
            final = last and c + 1 == NCH - 1
            return step_pairs((c + 1) % NCH, final)[:lead(final)]

        def pair_number(blk, c, pos):
            return blk * (NCH * PAIRS) + (PAIR0 + c * PAIRS + pos)

        def xb_slot(k):
            return PE_K.index(k) % XB

        def xb_before(k):
            nth = PE_K.index(k) - XB
            return nth < 0, PE_K[nth]

        def in_place(layer, k):
            return layer == 1 and k in PE_K and k in DVE_K

        def z_slot(c, pos):
            return (PAIR0 + c * PAIRS + pos) % ZS

        def split_pairs(early):
            return sorted(DVE_K if early else DVE_K + POOL_K)

        def split_tiles(k):
            return len([t for t in tiles_of(1, k) if t < T1 - 1])

        def split_number(blk, c, k, early):
            nth = split_pairs(early).index(k)
            if early:
                return c * len(DVE_K) + nth
            each = len(split_pairs(False))
            return blk * (NCH * each) + (c * each + nth - EARLY * len(POOL_K))

        def split_slot(c, k, early):
            return split_number(0 if early else 1, c, k, early) % HS

        assert (NCH * len(split_pairs(False))) % HS == 0

        def split_slot_before(c, k, early):
            pairs = split_pairs(early)
            nth = pairs.index(k) - HS
            if nth < 0 and c == EARLY and not early:
                assert split_pairs(True)[nth] <= pairs[nth]
            return nth < 0, pairs[nth]

        def tiles_of(layer, k):
            count = T0 if layer == 0 else T1
            return [t for t in (2 * k, 2 * k + 1) if t < count]

        @block.sync
        def _(sp):
            sp.dma_start(ids_all[:], A["ids"].rearrange("(n p) f -> p n f", p=P)).then_inc(ids_in, 16)
            sp.dma_start(look_ids, bass.AP(tensor=A["look_ids"].tensor, offset=A["look_ids"].offset,
                                           ap=[[0, LK], [1, NLOOK * P]])).then_inc(look_ids_in, 16)
            sp.dma_start(row_no[:], A["row_no"]).then_inc(look_ids_in, 16)

            def load_tables(g):
                for f in groups[g]:
                    to = xw_flat[0:LK, start_of[f]:start_of[f] + tiles_in[f] * D]
                    sp.dma_start(to, A[f"tbl_{f}"].rearrange("(p t) d -> p (t d)", p=LK)
                                 ).then_inc(table_in[g], 16)

            load_tables(0)
            full = (T1 - 1) * P
            sp.dma_start(w1[:, 0:T1 - 1, :],
                         A["W1"][0:full, :].rearrange("(t p) l -> p t l", p=P)).then_inc(w1_in, 16)
            sp.dma_start(w1[0:HK, T1 - 1, :], A["W1"][full:full + HK, :]).then_inc(w1_in, 16)
            load_tables(1)
            full = (T0 - 1) * FP
            for src, dst in ((A["w0_ij"], w0_ij), (A["w0_ji"], w0_ji)):
                sp.dma_start(dst[:, 0:T0 - 1, :],
                             src[0:full, :].rearrange("(t p) l -> p t l", p=FP)).then_inc(w0_in, 16)
                sp.dma_start(dst[0:LAST0, T0 - 1, :], src[full:full + LAST0, :]).then_inc(w0_in, 16)
            load_tables(2)
            sp.dma_start(wt1a[0:HK, :], A["W_top1"][0:HK, :]).then_inc(wt_in, 16)
            sp.dma_start(wt1a[HK:HK + NCTX, :], A["W_top1"][HK + L:HK + L + NCTX, :]).then_inc(wt_in, 16)
            sp.dma_start(wt1b, A["W_top1"][HK:HK + L, :]).then_inc(wt_in, 16)
            sp.dma_start(wt2, A["W_top2"].rearrange("(k p) n -> p k n", p=P)).then_inc(wt_in, 16)
            for g in range(3, NG):
                load_tables(g)
            sp.dma_start(ident[:], A["ident"]).then_inc(consts_in, 16)
            sp.dma_start(repeat0[:], A["repeat0"]).then_inc(consts_in, 16)
            sp.dma_start(shift0[:], A["shift0"].rearrange("p (t m) -> p t m", t=T0)).then_inc(consts_in, 16)
            sp.dma_start(spread1[:], A["spread1"].rearrange("p (t m) -> p t m", t=T1)).then_inc(consts_in, 16)
            sp.dma_start(wt3[:], A["W_top3"]).then_inc(top_in, 16)
            sp.dma_start(b1[:], A["b_top1"]).then_inc(top_in, 16)
            sp.dma_start(b2[:], A["b_top2"]).then_inc(top_in, 16)
            sp.dma_start(feat_a[HK:HK + NCTX, :], A["dense_ctx"]).then_inc(top_in, 16)

            def sp_wait(semaphore, value):
                sp.wait_ge(semaphore, value)
                sp.sem_inc(sp_turns, 1)

            def shift_chunk(blk, c, early):
                m = blk * NCH + c
                if not (early and c < 3):
                    sp_wait(xs_in, m * 48 - 96)
                sp_wait(x3_ready, m + 1)
                sp.dma_start(xt_scratch[c, :, :], x3[0:TWICE, c % 2, :]).then_inc(xt_out, 16)
                if early and c < 2:
                    sp_wait(xt_out, m * 16 + 16)
                    return
                if not early:
                    sp_wait(prod_done, pair_number(blk, c, 0) - 3 * PAIRS + PAIR0)
                sp_wait(xt_out, m * 16 + 16)
                for n in range(3):
                    rows = bass.AP(tensor=xt_scratch.tensor,
                                   offset=xt_scratch.offset + (c * TWICE + n) * CH,
                                   ap=[[CH, F], [3 * CH, T0], [1, CH]])
                    sp.dma_start(xs[n * F:(n + 1) * F, c % 2, :, :], rows).then_inc(xs_in, 16)

            def spread_pair(j, c):
                for half in range(2):
                    rows = bass.AP(tensor=xt_scratch.tensor,
                                   offset=xt_scratch.offset + (c * TWICE + 4 * DMA_K[j] + half) * CH,
                                   ap=[[0, HK], [2 * CH, 2], [1, CH]])
                    sp.dma_start(xw[half * HK:(half + 1) * HK, j, :, :], rows).then_inc(xw_in[j], 16)

            def step(blk, c, first, last):
                for j, k in enumerate(DMA_K):
                    if not (last and c == NCH - 1):
                        sp_wait(prod_done, pair_number(blk, c, PAIR0 + k) + 1)
                        spread_pair(j, (c + 1) % NCH)
                if not last or c == 0:
                    shift_chunk(blk + (c + AHEAD) // NCH, (c + AHEAD) % NCH, first and c == 0)

            shift_chunk(0, 0, True)
            for j in range(len(DMA_K)):
                spread_pair(j, 0)
            shift_chunk(0, 1, True)
            shift_chunk(0, 2, True)
            for c in range(NCH):
                step(0, c, True, False)
            with sp.Fori(1, NBLK - 1) as blk:
                for c in range(NCH):
                    step(blk, c, False, False)
            for c in range(NCH):
                step(NBLK - 1, c, False, True)
            sp.wait_ge(y_ready, 2)
            sp.dma_start(y_out.rearrange("b o -> o b"), y_row[:]).then_inc(y_out_done, 16)
            sp.wait_ge(y_out_done, 16)

        def part(n):
            return parts[:, :, n, :].rearrange("p d f -> p f d")

        @block.gpsimd
        def _(pool):
            def stand_alone():
                pool.sem_inc(pool_turns, 1)

            def next_ids(blk):
                pool.wait_ge(gathered, blk * (16 * F) - 16 * NLOOK)
                pool.wait_ge(split_step, blk * 4 - 2)
                stand_alone()
                nc.gpsimd.tensor_copy(ids_now[:], ids_all[:, bass.ds(blk, 1), :].rearrange(
                    "p o f -> p (o f)")).then_inc(ids_copied, 1)
                pool.wait_ge(ids_copied, blk + 1)
                stand_alone()

            def gather(fields):
                for f in fields:
                    nc.gpsimd.indirect_dma_start(
                        out=emb[:, f * D:(f + 1) * D], out_offset=None, in_=A[f"tbl_{f}"],
                        in_offset=bass.IndirectOffsetOnAxis(ap=ids_now[:, f:f + 1].bitcast(u32), axis=0),
                    ).then_inc(gathered, 16)

            def low_half(blk, c, k):
                final = blk is NBLK - 1 and c == NCH - 1
                pool.wait_ge(zh_done, split_number(blk, c, k, False) + 1)
                zs, hs = z_slot(c, k if final else PAIR0 + k), split_slot(c, k, False)
                n = split_tiles(k)
                nc.gpsimd.tensor_tensor(zl[:, hs, 0:n, :], z[:, zs, 0:n, :],
                                        zh[:, hs, 0:n, :].bitcast(fp32), ALU.subtract).then_inc(zl_pool, 1)

            def run_block(blk, gather_tail, gather_next):
                fields = list(range(HEAD, F)) if gather_tail else []
                for c in range(NCH):
                    for k in POOL_K:
                        low_half(blk, c, k)
                        if c == 1 and k == 5 and gather_next:
                            next_ids(blk + 2)
                            fields = list(range(HEAD))
                        some = 1 if k != POOL_K[-1] else 7 if c == 0 else 6
                        gather(fields[:some])
                        fields = fields[some:]
                assert not fields

            pool.wait_ge(ids_in, 16)
            nc.gpsimd.tensor_copy(ids_now[:], ids_all[:, 0, :]).then_inc(ids_copied, 1)
            pool.wait_ge(ids_copied, 1)
            gather(f for f in range(F) if f not in lookup)
            next_ids(1)
            gather(range(F))
            next_ids(2)
            ahead = HEAD - (NCH - EARLY) * (len(POOL_K) - 1)
            gather(range(ahead))
            for c in range(EARLY, NCH):
                for n, k in enumerate(POOL_K):
                    low_half(0, c, k)
                    if n + 1 < len(POOL_K):
                        gather(range(ahead, ahead + 1))
                        ahead += 1
            with pool.Fori(1, NBLK - 2) as blk:
                run_block(blk, True, True)
            run_block(NBLK - 2, True, False)
            run_block(NBLK - 1, False, False)

        @block.tensor
        def _(pe):
            def last_x3(c, last):
                return None if last and c + AHEAD - 1 >= NCH else c + AHEAD - 1

            def transpose_chunk(chunk_no, block_no, c):
                pe.wait_ge(split_step, block_no * 4 + 4)
                if not isinstance(chunk_no, int) or chunk_no:
                    pe.wait_ge(xparts_ready, chunk_no)
                for q in range(DC):
                    last = nc.tensor.transpose(
                        t_ps[0:FP, q * P:(q + 1) * P],
                        parts[:, c * DC + q, :, :].rearrange("p a f -> p (a f)"), ident[:])
                last.then_inc(transposed, 1)

            def make_x3(chunk_no, c):
                pe.wait_ge(xparts_ready, chunk_no + 1)
                pe.wait_ge(x3_ready, chunk_no)
                nc.tensor.matmul(x3_ps[0:FP, :], repeat0[:], xparts[:, c, :],
                                 start=True, stop=True).then_inc(x3_made, 1)

            def spread(c, k):
                slot = xb_slot(k)
                for n, t in enumerate(tiles_of(1, k)):
                    last = nc.tensor.matmul(xb[slot][:, n, :], spread1[:, t, :], xparts[:, c, :],
                                            start=True, stop=True)
                last.then_inc(spread_done, 1)

            def contract_0(k, zs):
                for n, t in enumerate(tiles_of(0, k)):
                    rows = FP if t < T0 - 1 else LAST0
                    last = nc.tensor.matmul(out0[:], w0[0:rows, t, :], z[0:rows, zs, n, :],
                                            start=(t == 0), stop=(t == T0 - 1))
                last.then_inc(pair_used, 1)

            def contract_1(k, zs, hs, dst):
                for n, t in enumerate(tiles_of(1, k)):
                    rows = P if t < T1 - 1 else HK
                    start, stop = t == 0, t == T1 - 1
                    if hs is None or t == T1 - 1:
                        last = nc.tensor.matmul(dst[:], w1[0:rows, t, :], z[0:rows, zs, n, :],
                                                start=start, stop=stop)
                    else:
                        for w, x in ((w1h, zh), (w1h, zl), (w1l, zh)):
                            last = nc.tensor.matmul(
                                dst[:], w[0:rows, t, :], x[0:rows, hs, n, :],
                                start=start and w is w1h and x is zh, stop=stop and w is w1l)
                last.then_inc(pair_used, 1)

            def step(blk, c, early, last):
                final = last and c == NCH - 1
                l0_pairs = 0 if final else PAIR0
                number = lambda pos: pair_number(blk, c, pos)

                def spread_ahead(k, nxt):
                    earlier, before = xb_before(k)
                    steps = (1 if nxt else 0) - (1 if earlier else 0)
                    if in_place(1, before):
                        pe.wait_ge(zl_dve, (blk * NCH + (c + steps)) * len(DVE_K) + DVE_K.index(before) + 1)
                    elif steps:
                        pe.wait_ge(prod_done, number(PAIR0 + before - PAIRS) + 1)
                    else:
                        pe.wait_ge(prod_done, number(l0_pairs + before) + 1)
                    spread((c + 1) % NCH if nxt else c, k)

                for pos, (layer, slot, k) in enumerate(step_pairs(c, final)):
                    ahead = pos + (PAIR0 if final else 0)
                    if ahead in PE_K[2:]:
                        spread_ahead(ahead, False)
                    if pos >= PAIRS - 2:
                        spread_ahead(PE_K[pos - (PAIRS - 2)], True)
                    if pos == 1 and last_x3(c, last) is not None:
                        make_x3(blk * NCH + (c + AHEAD - 1), (c + AHEAD - 1) % NCH)
                    if layer == 0:
                        if k == 0:
                            pe.wait_ge(h2_ready, (blk * NCH + c + 1) * 2)
                            pe.wait_ge(direct_done, blk * NCH + c + 1)
                        pe.wait_ge(prod_done, number(pos) + 1)
                        contract_0(k, z_slot(c, pos))
                    else:
                        if k == 0 and final:
                            pe.wait_ge(h2_ready, (blk * NCH + c + 1) * 2)
                            pe.wait_ge(direct_done, blk * NCH + c + 1)
                        elif k == 0:
                            pe.wait_ge(cur1_done, blk * NCH + c + 1)
                        split = k in split_pairs(early)
                        if not split:
                            pe.wait_ge(prod_done, number(pos) + 1)
                        elif k in DVE_K:
                            pe.wait_ge(zl_dve, (blk * NCH + c) * len(DVE_K) + (DVE_K.index(k) + 1))
                        else:
                            pe.wait_ge(zl_pool, (blk * NCH + c) * len(POOL_K)
                                       + (POOL_K.index(k) + 1 - EARLY * len(POOL_K)))
                        contract_1(k, z_slot(c, pos), split_slot(c, k, early) if split else None,
                                   out0 if final else out1)
                    if pos == PAIRS - 1 and (not last or c == 0):
                        transpose_chunk(blk * NCH + (c + AHEAD), blk + (c + AHEAD) // NCH,
                                        (c + AHEAD) % NCH)

            pe.sem_inc(transposed, 1)
            def shift_first(c, k):
                for n, t in enumerate(tiles_of(0, k)):
                    last = nc.tensor.matmul(xb[k % 2][0:FP, n, :], shift0[:, t, :], xparts[:, c, :],
                                            start=True, stop=True)
                last.then_inc(shifted, 1)

            for g, group in enumerate(groups):
                pe.wait_ge(one_hot_ready, g + 1)
                pe.wait_ge(table_low, 2 * g + 2)
                for n, f in enumerate(group):
                    tiles = tiles_in[f]
                    for t in range(tiles):
                        col = start_of[f] + t * D
                        last = nc.tensor.matmul(
                            look_bank[g][:, n * PARTS * D:(n + 1) * PARTS * D],
                            one_hot_tile(g, t)[:, n * P:(n + 1) * P],
                            table_parts.rearrange("p (m w) -> p m w", m=PARTS)[:, :, col:col + D],
                            start=(t == 0), stop=(t == tiles - 1))
                last.then_inc(look_done, 1)

            pe.wait_ge(consts_in, 64)
            transpose_chunk(0, 0, 0)
            make_x3(0, 0)
            shift_first(0, 0)
            shift_first(0, 1)
            transpose_chunk(1, 0, 1)
            pe.wait_ge(prod_done, 1)
            shift_first(0, 2)
            make_x3(1, 1)
            pe.wait_ge(prod_done, 2)
            shift_first(0, 3)
            pe.wait_ge(w0_ready, 2)
            contract_0(0, 0)
            for k in range(PAIR0):
                pe.wait_ge(prod_done, k + 3)
                shift_first(1, k)
                if k == 0:
                    transpose_chunk(2, 0, 2)
                if k + 1 < PAIR0:
                    contract_0(k + 1, k + 1)
            for n in range(2):
                pe.wait_ge(prod_done, 2 * PAIR0 + n - 1)
                spread(0, PE_K[n])
            pe.wait_ge(w1_in, 32)
            pe.wait_ge(w1_split, 2)
            for c in range(NCH):
                step(0, c, c < EARLY, False)
            with pe.Fori(1, NBLK - 1) as blk:
                for c in range(NCH):
                    step(blk, c, False, False)
            for c in range(NCH):
                step(NBLK - 1, c, False, True)

            n1, n2 = M1 // P, M2 // P

            def three_passes(dst, w_cols, high, low, rows, start, stop):
                for w, x in ((wth, high), (wth, low), (wtl, high)):
                    last = nc.tensor.matmul(dst, w[0:rows, w_cols], x, start=start and w is wth and x is high,
                                            stop=stop and w is wtl)
                return last

            def mlp1(half, m):
                if half:
                    pe.wait_ge(hid1_ready, 2 * (m + 1))
                fs = FEAT_SLOT[half]
                dst = xb[m // 2][:, m % 2, :]
                three_passes(dst, slice(m * P, (m + 1) * P), zh[0:HK + NCTX, fs, 0, :],
                             zl[0:HK + NCTX, fs, 0, :], HK + NCTX, True, False)
                three_passes(dst, slice(M1 + m * P, M1 + (m + 1) * P), zh[:, fs, 1, :],
                             zl[:, fs, 1, :], P, False, True).then_inc(mlp1_done, 1)

            def mlp2(half, m):
                if half:
                    pe.wait_ge(hid2_ready, m + 1)
                dst = (out0, out1)[m][:]
                for k in range(n1):
                    pe.wait_ge(hid1_low, half * n1 + k + 1)
                    col = 2 * M1 + k * M2 + m * P
                    hs = HID1_SLOT[half][k // 2]
                    last = three_passes(dst, slice(col, col + P), zh[:, hs, k % 2, :], zl[:, hs, k % 2, :],
                                        P, k == 0, k == n1 - 1)
                last.then_inc(mlp2_done, 1)

            pe.wait_ge(wt_split, 4)
            pe.wait_ge(top_in, 64)
            pe.wait_ge(feat_low, 2)
            for m in range(n1):
                mlp1(0, m)
            pe.wait_ge(feat_low, 4)
            for m in range(n1 // 2):
                mlp1(1, m)
            for m in range(n2):
                mlp2(0, m)
            for m in range(n1 // 2, n1):
                mlp1(1, m)
            for m in range(n2):
                mlp2(1, m)
            for half in range(2):
                pe.wait_ge(hid2_ready, n2 * (half + 1))
                dst = mlp3_ps[half][0:1, :]
                for k in range(n2):
                    last = nc.tensor.matmul(dst, wt3[:, k:k + 1], hid2[half][:, k, :],
                                            start=(k == 0), stop=(k == n2 - 1))
                last.then_inc(mlp3_done, 1)

        @block.scalar
        def _(act):
            def copy_xparts(chunk_no, c):
                act.wait_ge(transposed, chunk_no + 2)
                nc.scalar.copy(xparts[:, c, :], t_ps[0:FP, 0:CH]).then_inc(xparts_ready, 1)

            def copy_x3(chunk_no, c):
                act.wait_ge(x3_made, chunk_no + 1)
                nc.scalar.copy(x3[:, c % 2, :], x3_ps[0:FP, :]).then_inc(x3_ready, 1)

            def relu_next(pairs_used, slot):
                act.wait_ge(pair_used, pairs_used)
                for half in range(2):
                    nc.scalar.activation(h2[half * HK:(half + 1) * HK, slot, :], out0[HK:L, :],
                                         ACT.Relu).then_inc(h2_ready, 1)

            def split_part(blk, n):
                if n == 0:
                    act.wait_ge(gathered, (blk + 1) * (16 * F) - 16 * NLOOK)
                    act.wait_ge(transposed, blk * NCH + 1)
                    nc.scalar.copy(part(0), emb[:].rearrange("p (f d) -> p f d", f=F)).then_inc(split_step, 1)
                else:
                    act.wait_ge(split_step, blk * 4 + 2)
                    nc.scalar.copy(part(1), rest[:]).then_inc(split_step, 1)

            def high_half(blk, c, k, early, final):
                pos = k if final else PAIR0 + k
                act.wait_ge(prod_done, pair_number(blk, c, pos) + 1)
                earlier, before = split_slot_before(c, k, early)
                if not (early and c == 0 and earlier):
                    back = k - before + (PAIR0 + PAIR1 if earlier else 0) - (PAIR0 if earlier and final else 0)
                    act.wait_ge(pair_used, pair_number(blk, c, pos - back) + 1)
                hs = split_slot(c, k, early)
                src = xb[xb_slot(k)][:] if in_place(1, k) else z[:, z_slot(c, pos), :, :]
                n = split_tiles(k)
                nc.scalar.copy(zh[:, hs, 0:n, :], src[:, 0:n, :]).then_inc(zh_done, 1)

            def step(blk, c, early, last):
                final = last and c == NCH - 1
                for k in range(PAIR1):
                    if k in split_pairs(early):
                        high_half(blk, c, k, early, final)
                    if k == 2 and (not last or c + AHEAD - 1 < NCH):
                        copy_x3(blk * NCH + (c + AHEAD - 1), (c + AHEAD - 1) % NCH)
                    if c == 1 and not last and k in (2, 5):
                        split_part(blk + 1, 0 if k == 2 else 1)
                    if k == 4 and not final:
                        relu_next(pair_number(blk, c, PAIR0), (c + 1) % 2)
                if not last or c == 0:
                    chunk, to = blk * NCH + (c + AHEAD), (c + AHEAD) % NCH
                    copy_xparts(chunk, to)

            def table_highs(g):
                cols = group_cols(groups[g])
                act.wait_ge(table_in[g], 16 * len(groups[g]))
                nc.scalar.copy(table_part(0, cols), xw_flat[0:LK, cols]).then_inc(table_high, 1)
                act.wait_ge(table_low, 2 * g + 1)
                nc.scalar.copy(table_part(1, cols), table_rest[:, cols]).then_inc(table_high, 1)

            table_highs(0)
            table_highs(1)
            act.wait_ge(w1_in, 32)
            nc.scalar.copy(w1h[:], w1[:, 0:T1 - 1, :]).then_inc(w1_split, 1)
            for g in range(2, NG):
                table_highs(g)
            act.wait_ge(wt_in, 64)
            for rows, cols in ((HK + NCTX, slice(0, M1)), (P, slice(M1, None))):
                nc.scalar.copy(wth[0:rows, cols], wt[0:rows, cols]).then_inc(wt_split, 1)
            act.wait_ge(looked_up, NLOOK)
            split_part(0, 0)
            split_part(0, 1)
            copy_xparts(0, 0)
            copy_x3(0, 0)
            copy_xparts(1, 1)
            copy_x3(1, 1)
            copy_xparts(2, 2)
            relu_next(PAIR0, 0)
            for c in range(NCH):
                step(0, c, c < EARLY, False)
            with act.Fori(1, NBLK - 1) as blk:
                for c in range(NCH):
                    step(blk, c, False, False)
            for c in range(NCH):
                step(NBLK - 1, c, False, True)

            n1, n2 = M1 // P, M2 // P

            def relu_hid1(half, m):
                act.wait_ge(mlp1_done, half * n1 + m + 1)
                src, bias = xb[m // 2][:, m % 2, :], b1[:, m:m + 1]
                hs = HID1_SLOT[half][m // 2]
                if half and m == n1 // 2:
                    act.wait_ge(mlp2_done, n2)
                nc.scalar.activation(hid1[half][:, m, :], src, ACT.Relu, bias=bias).then_inc(hid1_ready, 1)
                nc.scalar.activation(zh[:, hs, m % 2, :], src, ACT.Relu, bias=bias).then_inc(hid1_ready, 1)

            def relu_hid2(half, m):
                act.wait_ge(mlp2_done, half * n2 + m + 1)
                nc.scalar.activation(hid2[half][:, m, :], (out0, out1)[m][:], ACT.Relu,
                                     bias=b2[:, m:m + 1]).then_inc(hid2_ready, 1)

            for half in range(2):
                cols, fs = slice(half * CH, (half + 1) * CH), FEAT_SLOT[half]
                act.wait_ge(feat_ready, NBLK * (half + 1))
                uses = [k for k in split_pairs(False) if split_slot(NCH - 1, k, False) == fs]
                act.wait_ge(pair_used, pair_number(NBLK - 1, NCH - 1, uses[-1]) + 1)
                nc.scalar.copy(zh[0:HK + NCTX, fs, 0, :], feat_a[:, cols]).then_inc(feat_high, 1)
                nc.scalar.copy(zh[:, fs, 1, :], feat_b[:, cols]).then_inc(feat_high, 1)
            for half, m in [(0, m) for m in range(n1)] + [(1, m) for m in range(n1 // 2)]:
                relu_hid1(half, m)
            for m in range(n2):
                relu_hid2(0, m)
            for m in range(n1 // 2, n1):
                relu_hid1(1, m)
            for m in range(n2):
                relu_hid2(1, m)
            for half in range(2):
                act.wait_ge(mlp3_done, half + 1)
                nc.scalar.copy(y_row[0:1, half * CH:(half + 1) * CH],
                               mlp3_ps[half][0:1, :]).then_inc(y_ready, 1)

        @block.vector
        def _(dve):
            dve.sem_inc(cur1_done, 1)

            def product(pair, number, zslot, l0_chunk, l1_chunk, free, opens=False):
                layer, c, k = pair
                n = len(tiles_of(layer, k))
                pairs = 1
                dst = z[:, zslot, 0:n, :]
                if layer == 0 and opens:
                    rows = FP if k < PAIR0 - 1 else LAST0
                    fixed = x3[0:rows, c % 2, :]
                    if k == 0:
                        dve.wait_ge(x3_ready, l0_chunk + 1)
                    own = xb[k % 2][0:rows, 0:n, :]
                    dve.wait_ge(shifted, c * PAIR0 + k + 1)
                elif layer == 0:
                    if k % 2:
                        return
                    rows, fixed, pairs, n = FP, x3[:, c % 2, :], 2, min(4, T0 - 2 * k)
                    dst = z[:, zslot:zslot + 2, :, :].rearrange("p s a n -> p (s a) n")[:, 0:n, :]
                    own = xs[0:rows, c % 2, 2 * k:2 * k + n, :]
                    if k == 0:
                        dve.wait_ge(x3_ready, l0_chunk + 1)
                        dve.wait_ge(xs_in, l0_chunk * 48 - 48)
                else:
                    rows, fixed = P, h2[:, c % 2, :]
                    if k == 0:
                        dve.wait_ge(h2_ready, l1_chunk * 2 + 2)
                    if k in DMA_K:
                        own = xw[:, DMA_K.index(k), :, :]
                        dve.wait_ge(xw_in[DMA_K.index(k)], l1_chunk * 32 + 32)
                    else:
                        own = xb[xb_slot(k)][:]
                        dve.wait_ge(spread_done, l1_chunk * len(PE_K) + (PE_K.index(k) + 1))
                if in_place(layer, k):
                    dst = own
                elif free:
                    dve.wait_ge(pair_used, number + pairs - ZS)
                nc.vector.tensor_tensor(dst[0:rows], own,
                                        fixed.unsqueeze(1).to_broadcast([rows, n, CH]),
                                        ALU.mult).then_inc(prod_done, pairs)

            def low_half(blk, c, k, early, final):
                dve.wait_ge(zh_done, split_number(blk, c, k, early) + 1)
                zs, hs = z_slot(c, k if final else PAIR0 + k), split_slot(c, k, early)
                src = xb[xb_slot(k)][:] if in_place(1, k) else z[:, zs, :, :]
                nc.vector.tensor_tensor(zl[:, hs, :, :], src,
                                        zh[:, hs, :, :].bitcast(fp32), ALU.subtract).then_inc(zl_dve, 1)

            def split_rest(blk, n):
                if n == 0:
                    dve.wait_ge(split_step, blk * 4 + 1)
                    nc.vector.tensor_tensor(rest[:], emb[:].rearrange("p (f d) -> p f d", f=F),
                                            part(0), ALU.subtract).then_inc(split_step, 1)
                else:
                    dve.wait_ge(split_step, blk * 4 + 3)
                    nc.vector.tensor_tensor(part(2), rest[:], part(1),
                                            ALU.subtract).then_inc(split_step, 1)

            def add_direct(blk, chunk_no, c, pairs_used):
                dve.wait_ge(pair_used, pairs_used)
                flat = sum_d[:].rearrange("l q b -> l (q b)")
                if c == 0:
                    nc.vector.tensor_scalar(flat, out0[0:HK, :], 0.0, None, ALU.max).then_inc(direct_done, 1)
                else:
                    dve.wait_ge(direct_done, chunk_no)
                    nc.vector.scalar_tensor_tensor(flat, out0[0:HK, :], 0.0, flat,
                                                   ALU.max, ALU.add).then_inc(direct_done, 1)
                if c == NCH - 1:
                    dve.wait_ge(direct_done, chunk_no + 1)
                    nc.vector.tensor_reduce(feat_a[0:HK, bass.ds(blk * P, P)],
                                            sum_d[:].rearrange("l q b -> l b q"),
                                            AX.X, ALU.add).then_inc(feat_ready, 1)

            def add_cur1(blk, chunk_no, c, pairs_used, src=out1):
                dve.wait_ge(pair_used, pairs_used)
                flat = sum_c[:].rearrange("l q b -> l (q b)")
                if c == 0:
                    nc.vector.tensor_scalar(flat, src[:], 0.0, None, ALU.max).then_inc(cur1_done, 1)
                else:
                    dve.wait_ge(cur1_done, chunk_no + 1)
                    nc.vector.scalar_tensor_tensor(flat, src[:], 0.0, flat,
                                                   ALU.max, ALU.add).then_inc(cur1_done, 1)
                if c == NCH - 1:
                    dve.wait_ge(cur1_done, chunk_no + 2)
                    nc.vector.tensor_reduce(feat_b[:, bass.ds(blk * P, P)],
                                            sum_c[:].rearrange("l q b -> l b q"),
                                            AX.X, ALU.add).then_inc(feat_ready, 1)

            def split_features(half):
                cols, fs = slice(half * CH, (half + 1) * CH), FEAT_SLOT[half]
                dve.wait_ge(feat_high, 2 * half + 2)
                for dst, high, src in ((zl[0:HK + NCTX, fs, 0, :], zh[0:HK + NCTX, fs, 0, :], feat_a),
                                       (zl[:, fs, 1, :], zh[:, fs, 1, :], feat_b)):
                    nc.vector.tensor_tensor(dst, src[:, cols], high.bitcast(fp32),
                                            ALU.subtract).then_inc(feat_low, 1)

            def step(blk, c, early, last):
                final = last and c == NCH - 1
                pairs = step_pairs(c, final)
                ahead = pairs + following(c, last)
                chunk = blk * NCH + c
                for pos in range(lead(final), len(ahead) + 1):
                    if pos < len(ahead):
                        nxt = pos >= len(pairs)
                        product(ahead[pos], pair_number(blk, c, pos), z_slot(c, pos),
                                chunk + (2 if nxt else 1), chunk + (1 if nxt else 0), True)
                    layer, slot, k = ahead[pos - 1]
                    if layer == 1 and k in DVE_K and (pos < len(ahead) or final):
                        low_half(blk, slot, k, early, final or slot != c)
                    if pos == PAIR0 + 5 and not final:
                        add_direct(blk if c < NCH - 1 else blk + 1, chunk + 1, (c + 1) % NCH,
                                   pair_number(blk, c, PAIR0))
                    if c == 1 and not last and pos in (PAIR0 + 4, PAIR0 + 7):
                        split_rest(blk + 1, 0 if pos == PAIR0 + 4 else 1)
                if final:
                    split_features(0)
                add_cur1(blk, chunk, c, pair_number(blk, c, len(pairs)), out0 if final else out1)

            def one_hots(g):
                tiles, n = tiles_in[groups[g][0]], len(groups[g]) * P
                ids = look_ids[:, lookup.index(groups[g][0]) * P:][:, 0:n]
                if g >= 2:
                    dve.wait_ge(look_done, g - 1)
                for t in range(tiles):
                    no = t if tiles == 8 else 8 + t
                    last = nc.vector.tensor_scalar(one_hot_tile(g, t), ids, row_no[:, no:no + 1],
                                                   None, ALU.is_equal)
                last.then_inc(one_hot_ready, 1)

            def table_lows(g, n):
                cols = group_cols(groups[g])
                dve.wait_ge(table_high, 2 * g + n + 1)
                if n:
                    nc.vector.tensor_tensor(table_part(2, cols), table_rest[:, cols], table_part(1, cols),
                                            ALU.subtract).then_inc(table_low, 1)
                else:
                    nc.vector.tensor_tensor(table_rest[:, cols], xw_flat[0:LK, cols],
                                            table_part(0, cols), ALU.subtract).then_inc(table_low, 1)

            def look_up(g):
                dve.wait_ge(look_done, g + 1)
                for n, f in enumerate(groups[g]):
                    nc.vector.tensor_reduce(
                        emb[:, f * D:(f + 1) * D],
                        look_bank[g][:, n * PARTS * D:(n + 1) * PARTS * D].rearrange("p (m d) -> p d m", d=D),
                        AX.X, ALU.add).then_inc(looked_up, 1)

            dve.wait_ge(look_ids_in, 32)
            one_hots(0)
            table_lows(0, 0)
            one_hots(1)
            table_lows(0, 1)
            table_lows(1, 0)
            dve.wait_ge(w0_in, 64)
            for half in range(2):
                to, frm = slice(half * HK, (half + 1) * HK), slice((1 - half) * HK, (2 - half) * HK)
                nc.vector.tensor_tensor(w0[:, 0:T0 - 1, to], w0_ij[:, 0:T0 - 1, frm],
                                        w0_ji[:, 0:T0 - 1, frm], ALU.add)
                last = nc.vector.tensor_tensor(w0[0:LAST0, T0 - 1, to], w0_ij[0:LAST0, T0 - 1, frm],
                                               w0_ji[0:LAST0, T0 - 1, frm], ALU.add)
                last.then_inc(w0_ready, 1)
            table_lows(1, 1)
            for g in range(2, NG):
                one_hots(g)
                table_lows(g, 0)
                look_up(g - 2)
                table_lows(g, 1)
            look_up(NG - 2)
            look_up(NG - 1)
            split_rest(0, 0)
            split_rest(0, 1)
            dve.wait_ge(wt_split, 2)
            for rows, cols in ((HK + NCTX, slice(0, M1)), (P, slice(M1, None))):
                nc.vector.tensor_tensor(wtl[0:rows, cols], wt[0:rows, cols], wth[0:rows, cols].bitcast(fp32),
                                        ALU.subtract).then_inc(wt_split, 1)
            opening = [(0, 0, k) for k in range(PAIR0)] + step_pairs(0, False)[:LEAD]
            for n, pair in enumerate(opening):
                if n == PAIR0:
                    dve.wait_ge(w1_split, 1)
                    nc.vector.tensor_tensor(w1l[:], w1[:, 0:T1 - 1, :], w1h[:].bitcast(fp32),
                                            ALU.subtract).then_inc(w1_split, 1)
                if n == 2 * PAIR0:
                    add_direct(0, 0, 0, PAIR0)
                product(pair, n, n % ZS, pair[1], 0, n >= ZS, opens=pair[0] == 0)
            for c in range(NCH):
                step(0, c, c < EARLY, False)
            with dve.Fori(1, NBLK - 1) as blk:
                for c in range(NCH):
                    step(blk, c, False, False)
            for c in range(NCH):
                step(NBLK - 1, c, False, True)

            n1 = M1 // P
            split_features(1)
            for half, m in [(half, m) for half in range(2) for m in range(n1)]:
                dve.wait_ge(hid1_ready, 2 * (half * n1 + m) + 2)
                hs = HID1_SLOT[half][m // 2]
                nc.vector.tensor_tensor(zl[:, hs, m % 2, :], hid1[half][:, m, :],
                                        zh[:, hs, m % 2, :].bitcast(fp32), ALU.subtract).then_inc(hid1_low, 1)


def kernel(**inputs):
    import numpy as np
    import ml_dtypes
    import concourse.bacc as bacc
    from concourse import mybir as mb
    from concourse.bass_utils import run_bass_kernel_spmd as run

    def c(a):
        return np.ascontiguousarray(np.asarray(a))

    field = np.arange(FP) % F
    one = ml_dtypes.bfloat16
    nth_shift = np.arange(FP) // F
    shift0 = np.stack([field[:, None] == (field + 3 * t + nth_shift)[None, :] % F for t in range(T0)], 1)
    spread1 = np.stack([field[:, None] == (2 * t + np.arange(L) // HK).clip(max=F - 1)[None, :]
                        for t in range(T1)], 1)
    s, i = np.meshgrid(np.arange(NSHIFT), np.arange(F), indexing="ij")
    j = (i + s) % F
    W0 = c(inputs["L0_rec_W0"])
    w0_ji = W0[(j * F + i).ravel()[F:]]

    rows_of = [inputs[f"tbl_{f}"].shape[0] for f in range(F)]
    lookup = sorted((f for f in range(F) if rows_of[f] in (8 * LK, 10 * LK)),
                    key=lambda f: rows_of[f])[:NLOOK]
    lane = np.arange(LK)[:, None]

    arrays = {
        "ids": c(inputs["ids"]),
        "look_ids": c(c(inputs["ids"])[0:P, lookup].T).reshape(-1),
        "row_no": np.concatenate([lane * 8 + np.arange(8), lane * 10 + np.arange(10)], 1).astype(np.float32),
        "ident": np.eye(P, dtype=one),
        "shift0": shift0.reshape(FP, T0 * FP).astype(one),
        "repeat0": (field[:, None] == field[None, :]).astype(one),
        "spread1": spread1.reshape(FP, T1 * L).astype(one),
        "w0_ij": W0[(i * F + j).ravel()],
        "w0_ji": np.concatenate([np.zeros((F, L), W0.dtype), w0_ji]),
        "W1": c(inputs["L0_rec_W1"]),
        "W_top1": c(inputs["W_top1"]),
        "W_top2": c(inputs["W_top2"]),
        "W_top3": c(c(inputs["W_top3"]).reshape(M2 // P, P).T),
        "b_top1": c(c(inputs["b_top1"]).reshape(M1 // P, P).T),
        "b_top2": c(c(inputs["b_top2"]).reshape(M2 // P, P).T),
        "dense_ctx": c(c(inputs["dense_ctx"]).T),
    }
    for f in range(F):
        arrays[f"tbl_{f}"] = c(inputs[f"tbl_{f}"])

    nc = bacc.Bacc("TRN2", target_bir_lowering=False, num_devices=1)
    A = {n: nc.dram_tensor(f"in_{n}", a.shape, mb.dt.from_np(a.dtype), kind="ExternalInput").ap()
         for n, a in arrays.items()}
    y = nc.dram_tensor("out_y", (B, 1), mb.dt.float32, kind="ExternalOutput").ap()
    xt_scratch = nc.dram_tensor("xt_scratch", (NCH, TWICE, CH), mb.dt.float32).ap()
    dlrm_tower(nc, A, xt_scratch, y)
    r = run(nc, [{f"in_{n}": a for n, a in arrays.items()}], core_ids=[0])
    return r.results[0]["out_y"]
```
